# Optimizing a Trainium2 kernel written in Bass

```python
import numpy as np
import jax
import jax.numpy as jnp

def _softmax(x, axis=-1):
    return jax.nn.softmax(x, axis=axis)

def _gelu(x):
    return jax.nn.gelu(x, approximate=True)

def _silu(x):
    return jax.nn.silu(x)

def _sigmoid(x):
    return jax.nn.sigmoid(x)

def _layernorm(x, axis=-1, eps=1e-05):
    m = jnp.mean(x, axis=axis, keepdims=True)
    v = jnp.var(x, axis=axis, keepdims=True)
    return (x - m) / jnp.sqrt(v + eps)

def _scatter_add(tgt, idx, src, axis=0):
    return tgt.at[idx].add(src)

def _segment_sum(src, seg, n):
    return jax.ops.segment_sum(src, seg, n)
kernel_name = 'mk_gps_d1_gnn_r32_ebbc3b'

def setup_inputs(seed: int=0):
    np.random.seed(seed)
    _w = jnp.asarray

    def _rec_inputs():
        import jax
        import jax.numpy as jnp
        _gk = jax.random.key(seed)
        x = -8.776e-05 + 1 * jax.random.normal(jax.random.fold_in(_gk, 1), (3125, 256), jnp.float32)
        src = jax.random.randint(jax.random.fold_in(_gk, 2), (50000,), 0, 3125, jnp.int32)
        dst = jnp.minimum((3125 * jax.random.uniform(jax.random.fold_in(_gk, 3), (50000,)) ** 2.0).astype(jnp.int32), 99999)
        _o = jnp.argsort(dst, stable=True)
        src = src[_o]
        dst = dst[_o]
        return (x, src, dst)
    x, src, dst = _rec_inputs()

    def _L0_gnn_setup():
        import jax, jax.numpy as jnp
        import numpy as np
        N_NODES = 625
        N_EDGES = 10000
        D = 256
        N_LAYERS = 3
        BN_EPS = 1e-05
        key = jax.random.key(seed)
        ks = jax.random.split(key, 5)
        x = jax.random.normal(ks[0], (N_NODES, D), dtype=jnp.float32)
        src = jax.random.randint(ks[1], (N_EDGES,), 0, N_NODES)
        dst = jax.random.randint(ks[2], (N_EDGES,), 0, N_NODES)
        scale = 1.0 / np.sqrt(D)
        thetas = jax.random.normal(ks[3], (N_LAYERS, D, D), dtype=jnp.float32) * scale
        phis = jax.random.normal(ks[4], (N_LAYERS, D, D), dtype=jnp.float32) * scale
        gammas = jnp.ones((N_LAYERS, D), dtype=jnp.float32)
        betas = jnp.zeros((N_LAYERS, D), dtype=jnp.float32)
        return {'x': x, 'src': src, 'dst': dst, 'thetas': thetas, 'phis': phis, 'gammas': gammas, 'betas': betas}
    _L0_gnn_all = _L0_gnn_setup()
    _L0_gnn_in = {k: v for k, v in _L0_gnn_all.items() if k in ('thetas', 'phis', 'gammas', 'betas')}
    del _L0_gnn_all

    def _L0_mix_setup():
        import jax, jax.numpy as jnp
        import numpy as np
        D_MODEL = 256
        NUM_HEADS = 8
        DEPTH = D_MODEL // NUM_HEADS
        B, L = (32, 128)

        def _feature_map(x):
            return jax.nn.elu(x) + 1.0
        key = jax.random.key(seed)
        ks = jax.random.split(key, 9)
        sc = 1.0 / np.sqrt(D_MODEL)
        return {'x': jax.random.normal(ks[0], (B, L, D_MODEL), dtype=jnp.float32), 'wq': jax.random.normal(ks[1], (D_MODEL, D_MODEL), dtype=jnp.float32) * sc, 'bq': jnp.zeros((D_MODEL,), dtype=jnp.float32), 'wk': jax.random.normal(ks[2], (D_MODEL, D_MODEL), dtype=jnp.float32) * sc, 'bk': jnp.zeros((D_MODEL,), dtype=jnp.float32), 'wv': jax.random.normal(ks[3], (D_MODEL, D_MODEL), dtype=jnp.float32) * sc, 'bv': jnp.zeros((D_MODEL,), dtype=jnp.float32), 'wo': jax.random.normal(ks[4], (D_MODEL, D_MODEL), dtype=jnp.float32) * sc, 'bo': jnp.zeros((D_MODEL,), dtype=jnp.float32)}
    _L0_mix_all = _L0_mix_setup()
    _L0_mix_in = {k: v for k, v in _L0_mix_all.items() if k in ('wq', 'bq', 'wk', 'bk', 'wv', 'bv', 'wo', 'bo')}
    del _L0_mix_all

    def _L0_ffn_setup():
        import jax, jax.numpy as jnp
        import numpy as np
        E = 8
        K = 2
        D = 256
        H = 512
        DOUT = 256
        EPS = 1e-05
        key = jax.random.key(seed)
        ks = jax.random.split(key, 9)
        s = 0.02
        return {'x': jax.random.normal(ks[0], (4, 256, D), jnp.float32), 'gamma': 1.0 + 0.05 * jax.random.normal(ks[1], (D,), jnp.float32), 'beta': 0.05 * jax.random.normal(ks[2], (D,), jnp.float32), 'Wr': 0.01 * jax.random.normal(ks[3], (D, E), jnp.float32), 'br': jnp.zeros((E,), jnp.float32), 'W1': s * jax.random.normal(ks[4], (E, D, H), jnp.float32), 'b1': s * jax.random.normal(ks[5], (E, H), jnp.float32), 'W2': s * jax.random.normal(ks[6], (E, H, DOUT), jnp.float32), 'b2': s * jax.random.normal(ks[7], (E, DOUT), jnp.float32)}
    _L0_ffn_all = _L0_ffn_setup()
    _L0_ffn_in = {k: v for k, v in _L0_ffn_all.items() if k in ('gamma', 'beta', 'Wr', 'br', 'W1', 'b1', 'W2', 'b2')}
    del _L0_ffn_all
    return {'x': x, 'src': src, 'dst': dst, 'L0_gnn_thetas': _L0_gnn_in['thetas'], 'L0_gnn_phis': _L0_gnn_in['phis'], 'L0_gnn_gammas': _L0_gnn_in['gammas'], 'L0_gnn_betas': _L0_gnn_in['betas'], 'L0_mix_wq': _L0_mix_in['wq'], 'L0_mix_bq': _L0_mix_in['bq'], 'L0_mix_wk': _L0_mix_in['wk'], 'L0_mix_bk': _L0_mix_in['bk'], 'L0_mix_wv': _L0_mix_in['wv'], 'L0_mix_bv': _L0_mix_in['bv'], 'L0_mix_wo': _L0_mix_in['wo'], 'L0_mix_bo': _L0_mix_in['bo'], 'L0_ffn_gamma': _L0_ffn_in['gamma'], 'L0_ffn_beta': _L0_ffn_in['beta'], 'L0_ffn_Wr': _L0_ffn_in['Wr'], 'L0_ffn_br': _L0_ffn_in['br'], 'L0_ffn_W1': _L0_ffn_in['W1'], 'L0_ffn_b1': _L0_ffn_in['b1'], 'L0_ffn_W2': _L0_ffn_in['W2'], 'L0_ffn_b2': _L0_ffn_in['b2']}

def reference(x, src, dst, L0_gnn_thetas, L0_gnn_phis, L0_gnn_gammas, L0_gnn_betas, L0_mix_wq, L0_mix_bq, L0_mix_wk, L0_mix_bk, L0_mix_wv, L0_mix_bv, L0_mix_wo, L0_mix_bo, L0_ffn_gamma, L0_ffn_beta, L0_ffn_Wr, L0_ffn_br, L0_ffn_W1, L0_ffn_b1, L0_ffn_W2, L0_ffn_b2):
    import jax
    import jax.numpy as jnp

    def _L0_gnn_ref(x, src, dst, thetas, phis, gammas, betas):
        import jax, jax.numpy as jnp
        import numpy as np
        N_NODES = 625
        N_EDGES = 10000
        D = 256
        N_LAYERS = 3
        BN_EPS = 1e-05
        N = x.shape[0]
        for l in range(thetas.shape[0]):
            xi = x[src]
            xj = x[dst]
            e = jax.nn.relu((xj - xi) @ thetas[l].T + xi @ phis[l].T)
            agg = jax.ops.segment_max(e, src, num_segments=N)
            agg = jnp.where(agg < -1e+30, 0.0, agg)
            mu = agg.mean(axis=0)
            var = agg.var(axis=0)
            x = jax.nn.relu((agg - mu) * jax.lax.rsqrt(var + BN_EPS) * gammas[l] + betas[l])
        return x

    def _L0_mix_ref(x, wq, bq, wk, bk, wv, bv, wo, bo):
        import jax, jax.numpy as jnp
        import numpy as np
        D_MODEL = 256
        NUM_HEADS = 8
        DEPTH = D_MODEL // NUM_HEADS
        B, L = (32, 128)

        def _feature_map(x):
            return jax.nn.elu(x) + 1.0
        b, l, _ = x.shape
        q = (x @ wq + bq).reshape(b, l, NUM_HEADS, DEPTH)
        k = (x @ wk + bk).reshape(b, l, NUM_HEADS, DEPTH)
        v = (x @ wv + bv).reshape(b, l, NUM_HEADS, DEPTH)
        q = _feature_map(q)
        k = _feature_map(k)
        kv = jnp.einsum('blhd,blhe->bhde', k, v)
        k_sum = jnp.sum(k, axis=1)
        qkv = jnp.einsum('blhd,bhde->blhe', q, kv)
        normalizer = jnp.einsum('blhd,bhd->blh', q, k_sum) + 1e-06
        out = qkv / normalizer[..., None]
        out = out.reshape(b, l, D_MODEL)
        return out @ wo + bo

    def _L0_ffn_ref(x, gamma, beta, Wr, br, W1, b1, W2, b2):
        import jax, jax.numpy as jnp
        import numpy as np
        E = 8
        K = 2
        D = 256
        H = 512
        DOUT = 256
        EPS = 1e-05
        mu = jnp.mean(x, axis=-1, keepdims=True)
        var = jnp.mean(jnp.square(x - mu), axis=-1, keepdims=True)
        xn = (x - mu) * jax.lax.rsqrt(var + EPS) * gamma + beta
        logits = jnp.einsum('bsd,de->bse', xn, Wr) + br
        top_vals, top_idx = jax.lax.top_k(logits, K)
        w = jax.nn.softmax(top_vals, axis=-1)
        w_full = jnp.einsum('bsk,bske->bse', w, jax.nn.one_hot(top_idx, E, dtype=w.dtype))
        y = jnp.zeros(x.shape[:-1] + (DOUT,), x.dtype)
        for e in range(E):
            h = jax.nn.gelu(jnp.einsum('bsd,dh->bsh', xn, W1[e]) + b1[e], approximate=False)
            y_e = jnp.einsum('bsh,hd->bsd', h, W2[e]) + b2[e]
            y = y + y_e * w_full[..., e, None]
        return y
    xn = _layernorm(x, axis=-1)
    x = x + _L0_gnn_ref(xn, src, dst, L0_gnn_thetas, L0_gnn_phis, L0_gnn_gammas, L0_gnn_betas) + _L0_mix_ref(xn[None], L0_mix_wq, L0_mix_bq, L0_mix_wk, L0_mix_bk, L0_mix_wv, L0_mix_bv, L0_mix_wo, L0_mix_bo)[0]
    x = x + _L0_ffn_ref(_layernorm(x, axis=-1)[None], L0_ffn_gamma, L0_ffn_beta, L0_ffn_Wr, L0_ffn_br, L0_ffn_W1, L0_ffn_b1, L0_ffn_W2, L0_ffn_b2)[0]
    return x

_drawn_inputs = setup_inputs


def setup_inputs(seed=0):
    import zlib

    import numpy as np

    out = dict(_drawn_inputs(seed))
    spreads = {'L0_gnn_gammas': (1.0, 0.2),
     'L0_gnn_betas': (0.0, 0.1),
     'L0_mix_bq': (0.0, 2.0),
     'L0_mix_bk': (0.0, 2.0),
     'L0_mix_bv': (0.0, 0.1),
     'L0_mix_bo': (0.0, 0.1),
     'L0_ffn_br': (0.0, 0.1)}
    factors = {'L0_mix_wq': 8.0,
     'L0_mix_wk': 7.467,
     'L0_mix_wv': 3.628,
     'L0_ffn_gamma': 7.822,
     'L0_ffn_beta': 6.592,
     'L0_ffn_b1': 8.0,
     'L0_ffn_b2': 5.477}
    for name, (base, spread) in spreads.items():
        noise = np.random.default_rng([zlib.crc32(name.encode()), seed]).standard_normal(out[name].shape)
        drawn = base * np.exp(spread * noise) if base else spread * noise
        out[name] = jnp.asarray(drawn.astype(out[name].dtype))
    for name, factor in factors.items():
        out[name] = (out[name] * factor).astype(out[name].dtype)
    return out
```

```python
from contextlib import ExitStack

import numpy as np

import concourse.bass as bass
from concourse import mybir

F32 = mybir.dt.float32
F16 = mybir.dt.float16
I32 = mybir.dt.int32
U32 = mybir.dt.uint32
ALU = mybir.AluOpType
ACT = mybir.ActivationFunctionType
AX_X = mybir.AxisListType.X
RMAX = bass.bass_isa.ReduceOp.max

P = 128
N = 3125
D = 256
H2 = D // P
NT = -(-N // P)
NP = NT * P
LAST = N - (NT - 1) * P
NE = 50000
EB = 125
NB = NE // EB
CB = 20
NC = NB // CB
LAYERS = 3
MID = NP // 2
ROWS = NP + 1
K = 8
WIN = 56 * K
NW = -(-(NE + NE // P + 2 * NT) // WIN)
NEG = -3.0e38
DEGCAP = 4095
HEADS = 8
DH = D // HEADS
EXPERTS = 8
HID = 512
EPS = 1e-5
U = 5


def build(nc, t, out):
    ctx = ExitStack()
    with ctx:
        def sb(name, shape, dt=F32):
            return ctx.enter_context(nc.sbuf_tensor(name, shape, dt))

        phase_sems = []

        def sem(name):
            phase_sems.append(nc.alloc_semaphore(name=name))
            return phase_sems[-1]

        gather_sems = {}

        def gsem(name):
            if name not in gather_sems:
                gather_sems[name] = nc.alloc_semaphore(name=name)
            return gather_sems[name]

        def end_phase():
            with nc.Block() as block:
                @block.gpsimd
                def _(pool):
                    for s in phase_sems:
                        pool.sem_clear(s)
            for s in phase_sems:
                nc.release_semaphore(s)
            phase_sems.clear()

        ps = [ctx.enter_context(nc.psum_tensor(f"bank{i}", [P, 512], F32)) for i in range(8)]

        def dram(name, shape, dt=F32):
            return nc.dram_tensor(name, shape, dt).ap()

        x_perm = dram("x_perm", (NP, D + 1))
        lo_dram = dram("lo_dram", (NE,), F16)
        key_dram = dram("key_dram", (P, NT))
        table_dram = dram("table_dram", (NW, P, WIN), I32)
        tile_dram = dram("tile_dram", (NW, WIN), I32)
        a_rows = [dram(f"a_rows{l}", (ROWS, D)) for l in range(LAYERS)]

        held = ctx.enter_context(nc.semaphore("held"))

        def hold(eng, semaphore, value):
            eng.wait_ge(semaphore, value)
            eng.sem_inc(held, 1)

        iota = sb("iota", [P, WIN], F16)
        iota_p = sb("iota_p", [P, 1])
        ident = sb("ident", [P, P])
        rowid = sb("rowid", [P, NT], I32)
        nodeid = sb("nodeid", [P, NT], I32)
        xin = sb("xin", [P, NT, D + 1])
        nwin = sb("nwin", [1, 1], I32)
        nstep = sb("nstep", [1, P], I32)
        slotbase = sb("slotbase", [P, NT + 1])

        c2 = ExitStack()
        ctx.callback(c2.close)

        def sb2(name, shape, dt=F32):
            return c2.enter_context(nc.sbuf_tensor(name, shape, dt))

        oh_hi = sb2("oh_hi", [EB, NB, NT], F16)
        dv_e = sb2("dv_e", [EB, NB])
        hist = sb2("hist", [P, NB, NT], F16)
        nbase = sb2("nbase", [P, NT])
        q_h = sb2("q_h", [P, NT], F16)

        with ExitStack() as c1:
            def sb1(name, shape, dt=F32):
                return c1.enter_context(nc.sbuf_tensor(name, shape, dt))
            q4 = NB // 100
            src_r = sb1("src_r", [100, q4, EB], I32)
            dst_r = sb1("dst_r", [100, q4, EB], I32)
            lo_i = sb1("lo_i", [100, q4, EB], I32)
            hi_i = sb1("hi_i", [100, q4, EB], I32)
            lo_f = sb1("lo_f", [100, q4, EB])
            hi_f = sb1("hi_f", [100, q4, EB])
            dv_f = sb1("dv_f", [100, q4, EB])
            dv_g = sb1("dv_g", [100, q4, EB])
            lo_h = sb1("lo_h", [100, q4, EB], F16)
            lo_e = sb1("lo_e", [EB, NB], F16)
            hi_e = sb1("hi_e", [EB, NB], F16)
            oh_lo = [sb1(f"oh_lo{i}", [EB, CB, P], F16) for i in range(2)]
            zero = sb1("zero", [P, P + NT], F16)
            deg = sb1("deg", [P, NT])
            iota_i = sb1("iota_i", [P, NT], I32)
            node_f = sb1("node_f", [P, NT])
            key = sb1("key", [P, NT])
            key_all = sb1("key_all", [P, NP])
            rank = sb1("rank", [P, NT])
            junk = sb1("junk", [P, NP])
            rank_i = sb1("rank_i", [P, NT], I32)
            tq_i = sb1("tq_i", [P, 2, NT], I32)
            tq_f = sb1("tq_f", [P, 2, NT])
            idv = sb1("idv", [P, NT], I32)
            ge = sb1("ge", [P, NT])
            idf = sb1("idf", [P, NT])
            sel3 = sb1("sel3", [P, NT, NT])
            tmax = sb1("tmax", [P, NT])
            tmax_all = sb1("tmax_all", [P, NT])
            zeros25 = sb1("zeros25", [P, NT])
            steps_f = sb1("steps_f", [1, P])
            small = sb1("small", [1, 4])
            small_i = sb1("small_i", [1, 2], I32)
            wf = sb1("wf", [1, P])

            loaded, loaded_x = sem("loaded"), sem("loaded_x")
            made = sem("made")
            dve1 = sem("dve1")
            turned, oh_ready, oh_used = sem("turned"), sem("oh_ready"), sem("oh_used")
            hist_ready, hist_used = sem("hist_ready"), sem("hist_used")
            lo_stored, key_stored, key_loaded = sem("lo_stored"), sem("key_stored"), sem("key_loaded")
            degree_ready = sem("degree_ready")
            tmax_ready, tmax_done = sem("tmax_ready"), sem("tmax_done")
            scattered = gsem("scattered")

            n_consts = 8
            pad_cleared, lo_made, key_made, places_made = (sem("pad_cleared"), sem("lo_made"), sem("key_made"),
                                                           sem("places_made"))
            columns_made = sem("columns_made")
            with nc.Block() as block:
                @block.gpsimd
                def _(pool):
                    pool.iota(iota[:], [[1, WIN]], base=0, channel_multiplier=0,
                              allow_small_or_imprecise_dtypes=True).then_inc(made, 1)
                    pool.iota(iota_p[:], [[0, 1]], base=0, channel_multiplier=1,
                              allow_small_or_imprecise_dtypes=True).then_inc(made, 1)
                    pool.iota(iota_i[:], [[P, NT]], base=0, channel_multiplier=1).then_inc(made, 1)
                    pool.iota(wf[:], [[WIN // K, P]], base=0, channel_multiplier=0,
                              allow_small_or_imprecise_dtypes=True).then_inc(made, 1)
                    pool.memset(ident[:], 0.0).then_inc(made, 1)
                    pool.wait_ge(made, 5)
                    pool.affine_select(out=ident[:], in_=ident[:], compare_op=ALU.not_equal, fill=1.0, base=0,
                                       pattern=[[-1, P]], channel_multiplier=1).then_inc(made, 1)
                    pool.memset(zero[:], 0.0).then_inc(made, 1)
                    pool.memset(zeros25[:], 0.0).then_inc(made, 1)
                    pool.wait_ge(tmax_ready, 1)
                    pool.partition_all_reduce(tmax_all[:], tmax[:], P, RMAX).then_inc(tmax_done, 1)
                    pool.wait_ge(loaded_x, 32)
                    pool.wait_ge(places_made, 1)
                    for h in range(NT):
                        pool.indirect_dma_start(
                            x_perm, bass.IndirectOffsetOnAxis(ap=rank_i[:, h:h + 1].bitcast(U32), axis=0),
                            xin[:, h, :], None).then_inc(scattered, 16)
                    pool.wait_ge(scattered, 16 * NT)

                @block.sync
                def _(sp):
                    r = "(g r e) -> r g e"
                    sp.dma_start(src_r[:], t["src"].rearrange(r, g=q4, r=100)).then_inc(loaded, 16)
                    sp.dma_start(dst_r[:], t["dst"].rearrange(r, g=q4, r=100)).then_inc(loaded, 16)
                    sp.dma_start(xin[:, 0:NT - 1, 0:D],
                                 t["x"][0:(NT - 1) * P, :].rearrange("(h p) d -> p h d", p=P)).then_inc(loaded_x, 16)
                    sp.wait_ge(pad_cleared, 1)
                    sp.dma_start(xin[0:LAST, NT - 1, 0:D], t["x"][(NT - 1) * P:N, :]).then_inc(loaded_x, 16)
                    sp.wait_ge(lo_made, 1)
                    sp.dma_start(lo_dram.rearrange(r, g=q4, r=100), lo_h[:]).then_inc(lo_stored, 16)
                    sp.wait_ge(key_made, 1)
                    sp.dma_start(key_dram, key[:]).then_inc(key_stored, 16)
                    sp.wait_ge(key_stored, 16)
                    sp.dma_start(key_all[:], key_dram.rearrange("p t -> (p t)").partition_broadcast(P)
                                 ).then_inc(key_loaded, 16)
                    sp.wait_ge(lo_stored, 16)

                @block.tensor
                def _(pe):
                    pe.wait_ge(made, 6)
                    for i, (a, bank) in enumerate(((lo_f, 0), (hi_f, 1), (dv_f, 2))):
                        pe.wait_ge(columns_made, i + 1)
                        for g in range(q4):
                            mm = pe.transpose(ps[bank][0:EB, g * 100:(g + 1) * 100], a[:, g, :], ident[0:100, 0:100])
                        mm.then_inc(turned, 1)
                    pe.wait_ge(made, n_consts)
                    pe.matmul(ps[3][:, 0:NT], zero[:, 0:P], zero[:, P:P + NT], start=True, stop=False,
                              skip_group_check=True)
                    with pe.Fori(0, NC // 2) as j:
                        for i in range(2):
                            pe.wait_ge(oh_ready, 2 * j + i + 1)
                            pe.wait_ge(hist_used, 2 * j + i + 1)
                            for b in range(CB):
                                c = (2 * j + i) * CB + b
                                rhs = oh_hi[:, bass.ds(c, 1), :].rearrange("e a b -> e (a b)")
                                pe.matmul(ps[3][:, 0:NT], oh_lo[i][:, b, :], rhs,
                                          start=False, stop=False, skip_group_check=True)
                                mm = pe.matmul(ps[4 + i][:, b * NT:(b + 1) * NT], oh_lo[i][:, b, :], rhs,
                                               start=True, stop=True, skip_group_check=True)
                            mm.then_inc(hist_ready, 1)
                    pe.matmul(ps[3][:, 0:NT], zero[:, 0:P], zero[:, P:P + NT], start=False, stop=True,
                              skip_group_check=True).then_inc(degree_ready, 1)

                @block.scalar
                def _(act):
                    act.sem_inc(hist_used, 2)
                    with act.Fori(0, NC // 2) as j:
                        for i in range(2):
                            act.wait_ge(hist_ready, 2 * j + i + 1)
                            act.copy(hist[:, bass.ds((2 * j + i) * CB, CB), :].rearrange("p a b -> p (a b)"),
                                     ps[4 + i][:, 0:CB * NT]).then_inc(hist_used, 1)

                @block.vector
                def _(dve):
                    count = [0]

                    def step(ins, made=None):
                        ins.then_inc(dve1, 1)
                        count[0] += 1
                        dve.wait_ge(dve1, count[0])
                        if made is not None:
                            dve.sem_inc(made, 1)

                    dve.memset(junk[:], 0.0)
                    step(dve.memset(xin[:, NT - 1, :], 0.0), pad_cleared)
                    dve.wait_ge(loaded, 32)
                    dve.tensor_scalar(lo_i[:], src_r[:], P - 1, None, ALU.bitwise_and)
                    step(dve.tensor_scalar(hi_i[:], src_r[:], 7, None, ALU.logical_shift_right))
                    step(dve.tensor_copy(lo_h[:], lo_i[:]), lo_made)
                    step(dve.tensor_copy(lo_f[:], lo_i[:]), columns_made)
                    step(dve.tensor_copy(hi_f[:], hi_i[:]), columns_made)
                    step(dve.tensor_scalar(dv_g[:], dst_r[:], float(MID), None, ALU.is_ge))
                    step(dve.scalar_tensor_tensor(dv_f[:], dst_r[:], float(MID), dv_g[:], ALU.subtract, ALU.add), columns_made)
                    dve.wait_ge(turned, 3)
                    dve.tensor_copy(lo_e[:], ps[0][0:EB, 0:NB])
                    dve.tensor_copy(dv_e[:], ps[2][0:EB, 0:NB])
                    step(dve.tensor_copy(hi_e[:], ps[1][0:EB, 0:NB]))
                    dve.wait_ge(made, n_consts)
                    step(dve.tensor_tensor(oh_hi[:], iota[0:EB, 0:NT].unsqueeze(1).broadcast_to([EB, NB, NT]),
                                           hi_e[:].unsqueeze(2).broadcast_to([EB, NB, NT]), ALU.is_equal))
                    with dve.Fori(0, NC // 2) as j:
                        for i in range(2):
                            dve.wait_ge(hist_used, 2 * j + i + 1)
                            dve.tensor_tensor(
                                oh_lo[i][:], iota[0:EB, 0:P].unsqueeze(1).broadcast_to([EB, CB, P]),
                                lo_e[:, bass.ds((2 * j + i) * CB, CB)].unsqueeze(2).broadcast_to([EB, CB, P]),
                                ALU.is_equal).then_inc(oh_ready, 1)
                    dve.wait_ge(degree_ready, 1)
                    dve.tensor_copy(node_f[:], iota_i[:])
                    step(dve.tensor_copy(deg[:], ps[3][:, 0:NT]))
                    step(dve.tensor_scalar(key[:], deg[:], float(DEGCAP), float(DEGCAP + 1), ALU.min, ALU.mult))
                    step(dve.tensor_tensor(key[:], key[:], node_f[:], ALU.subtract), key_made)
                    step(dve.tensor_scalar(ge[:], node_f[:], float(MID), None, ALU.is_ge))
                    step(dve.tensor_tensor(idf[:], node_f[:], ge[:], ALU.add))
                    step(dve.tensor_copy(idv[:], idf[:]))
                    step(dve.tensor_copy(xin[:, :, D:D + 1].bitcast(I32), idv[:].unsqueeze(2)))
                    dve.wait_ge(key_loaded, 16)
                    for h in range(NT):
                        ins = dve.tensor_scalar(junk[:], key_all[:], key[:, h:h + 1], None, ALU.is_gt, ALU.add,
                                                accum_out=rank[:, h:h + 1])
                        step(ins)
                    step(dve.tensor_copy(rank_i[:], rank[:]), places_made)
                    step(dve.tensor_scalar(tq_i[:, 0, :], rank_i[:], 7, None, ALU.logical_shift_right))
                    step(dve.tensor_scalar(tq_i[:, 1, :], rank_i[:], P - 1, None, ALU.bitwise_and))
                    step(dve.tensor_copy(tq_f[:], tq_i[:]))
                    step(dve.tensor_copy(q_h[:], tq_f[:, 1, :]))
                    shape = [P, NT, NT]
                    step(dve.tensor_tensor(sel3[:], iota[:, 0:NT].unsqueeze(2).broadcast_to(shape),
                                           tq_f[:, 0, :].unsqueeze(1).broadcast_to(shape), ALU.is_equal))
                    step(dve.tensor_tensor(sel3[:], sel3[:], deg[:].unsqueeze(1).broadcast_to(shape), ALU.mult))
                    step(dve.tensor_reduce(tmax[:], sel3[:], AX_X, ALU.max))
                    dve.sem_inc(tmax_ready, 1)
                    dve.wait_ge(tmax_done, 1)
                    step(dve.memset(slotbase[:, 0:1], 0.0))
                    step(dve.tensor_tensor_scan(slotbase[:, 1:NT + 1], tmax_all[:], zeros25[:], 0.0, ALU.add, ALU.add))
                    step(dve.tensor_tensor(sel3[:], iota[:, 0:NT].unsqueeze(1).broadcast_to(shape),
                                           tq_f[:, 0, :].unsqueeze(2).broadcast_to(shape), ALU.is_equal))
                    step(dve.tensor_tensor(sel3[:], sel3[:], slotbase[:, 0:NT].unsqueeze(1).broadcast_to(shape), ALU.mult))
                    step(dve.tensor_reduce(nbase[:], sel3[:], AX_X, ALU.add))
                    spw = WIN // K
                    step(dve.tensor_scalar(small[:, 0:1], slotbase[0:1, NT:NT + 1], float(K - 1), None, ALU.add))
                    step(dve.tensor_copy(small_i[:, 0:1], small[:, 0:1]))
                    step(dve.tensor_scalar(small_i[:, 1:2], small_i[:, 0:1], K.bit_length() - 1, None,
                                           ALU.logical_shift_right))
                    step(dve.tensor_copy(small[:, 0:1], small_i[:, 1:2]))
                    step(dve.tensor_scalar(steps_f[:], wf[:], small[:, 0:1], None, ALU.is_lt))
                    step(dve.tensor_reduce(small[:, 1:2], steps_f[:], AX_X, ALU.add))
                    step(dve.tensor_copy(nwin[:], small[:, 1:2]))
                    step(dve.tensor_scalar(wf[:], wf[:], small[:, 0:1], -1.0, ALU.subtract, ALU.mult))
                    step(dve.tensor_scalar(wf[:], wf[:], 1.0, float(spw), ALU.max, ALU.min))
                    step(dve.tensor_copy(nstep[:], wf[:]))

        end_phase()

        with ExitStack() as c3:
            def sb3(name, shape, dt=F32):
                return c3.enter_context(nc.sbuf_tensor(name, shape, dt))
            xpre = sb3("xpre", [P, NB, NT])
            lo_bc = [sb3(f"lo_bc{i}", [P, CB * EB], F16) for i in range(2)]
            lot = [sb3(f"lot{i}", [P, CB, EB], F16) for i in range(2)]
            xc = sb3("xc", [P, CB * NT])
            xw = [sb3(f"xw{i}", [P, CB, NT], F16) for i in range(2)]
            earlier = sb3("earlier", [EB, EB], F16)
            eqm = [sb3(f"eqm{i}", [EB, 4, EB], F16) for i in range(2)]
            rm = [sb3(f"rm{i}", [EB, CB // 2, 2, NT]) for i in range(2)]
            gq = [sb3(f"gq{i}", [EB, CB, 2]) for i in range(2)]
            RG = 5
            ohq = [sb3(f"ohq{i}", [EB, P], F16) for i in range(RG)]
            ohg = [sb3(f"ohg{i}", [EB, WIN], F16) for i in range(RG)]
            wshift = sb3("wshift", [P, 1])
            zscan = sb3("zscan", [P, 1])
            zero2 = sb3("zero2", [EB, WIN], F16)
            tab_f = sb3("tab_f", [P, WIN])
            tab_i = sb3("tab_i", [P, WIN], I32)
            gnum_i = sb3("gnum_i", [WIN // 4, 4], I32)
            gnum = sb3("gnum", [WIN // 4, 4])
            tcmp = sb3("tcmp", [WIN // 4, 4, NT - 1])
            tsum = sb3("tsum", [WIN // 4, 4])
            tof = sb3("tof", [WIN // 4, 4], I32)

            made2, dve2 = sem("made2"), sem("dve2")
            lo_loaded = [sem(f"lo_loaded{i}") for i in range(2)]
            lot_ready, eq_ready, eq_masked, xq_ready = sem("lot_ready"), sem("eq_ready"), sem("eq_masked"), sem("xq_ready")
            r_ready, r_read = sem("r_ready"), sem("r_read")
            hot_ready, hot_used = sem("hot_ready"), sem("hot_used")
            win_done, win_read = sem("win_done"), sem("win_read")
            table_chain = sem("table_chain")
            table_made, table_stored = sem("table_made"), sem("table_stored")

            with nc.Block() as block:
                @block.gpsimd
                def _(pool):
                    pool.iota(gnum_i[:], [[1, 4]], base=0, channel_multiplier=4).then_inc(made2, 1)
                    pool.memset(earlier[:], 1.0).then_inc(made2, 1)
                    pool.wait_ge(made2, 2)
                    pool.affine_select(out=earlier[:], in_=earlier[:], compare_op=ALU.is_gt, fill=0.0, base=0,
                                       pattern=[[1, EB]], channel_multiplier=-1).then_inc(made2, 1)

                @block.sync
                def _(sp):
                    windows = sp.value_load(nwin[0:1, 0:1], min_val=1, max_val=NW)
                    with sp.Fori(0, windows) as w:
                        with sp.Fori(0, NC // 2) as j:
                            for i in range(2):
                                hold(sp, lot_ready, w * NC + 2 * j + i + 1)
                                sp.dma_start(lo_bc[i][:], lo_dram[bass.ds((2 * j + i) * (CB * EB), CB * EB)]
                                             .partition_broadcast(P)).then_inc(lo_loaded[i], 16)
                        hold(sp, table_made, w + 1)
                        sp.dma_start(table_dram[bass.ds(w, 1)].rearrange("o p g -> (o p) g"), tab_i[:]
                                     ).then_inc(table_stored, 16)
                        sp.dma_start(tile_dram[bass.ds(w, 1)].rearrange("o (p g) -> (o p) g", g=4), tof[:]
                                     ).then_inc(table_stored, 16)
                        hold(sp, table_stored, w * 32 + 32)

                @block.tensor
                def _(pe):
                    windows = pe.value_load(nwin[0:1, 0:1], min_val=1, max_val=NW)
                    with pe.Fori(0, windows) as w:
                        pe.wait_ge(win_read, w + 1)
                        pe.matmul(ps[7][:, 0:WIN], zero2[:, 0:P], zero2[:, 0:WIN], start=True, stop=False,
                                  skip_group_check=True)
                        with pe.Fori(0, NC // 2) as j:
                            for i in range(2):
                                cc = w * NC + 2 * j + i
                                pe.wait_ge(lot_ready, cc + 3)
                                pe.wait_ge(r_read, cc + 1)
                                for b in range(CB):
                                    r = ps[2 + 2 * i + b // 10][0:EB, (b % 10) * 2 * NT:(b % 10 + 1) * 2 * NT]
                                    pe.matmul(r[:, 0:NT], lot[i][:, b, :], xw[i][:, b, :], start=b % 10 == 0,
                                              stop=False, skip_group_check=True)
                                    pe.matmul(r[:, NT:2 * NT], lot[i][:, b, :], q_h[:], start=False, stop=False,
                                              skip_group_check=True)
                                for qd in range(CB // 4 + 1):
                                    if qd < CB // 4:
                                        if qd >= 2:
                                            pe.wait_ge(eq_masked, cc * (CB // 4) + qd - 1)
                                        for b in range(4):
                                            l = lot[i][:, 4 * qd + b, :]
                                            mm = pe.matmul(ps[qd % 2][0:EB, b * EB:(b + 1) * EB], l, l,
                                                           start=True, stop=True, skip_group_check=True)
                                        mm.then_inc(eq_ready, 1)
                                    if qd >= 1:
                                        pe.wait_ge(eq_masked, cc * (CB // 4) + qd)
                                        for b in range(4 * qd - 4, 4 * qd):
                                            r = ps[2 + 2 * i + b // 10][0:EB, (b % 10) * 2 * NT:(b % 10) * 2 * NT + NT]
                                            rhs = oh_hi[:, bass.ds((2 * j + i) * CB + b, 1), :].rearrange("e a b -> e (a b)")
                                            mm = pe.matmul(r, eqm[(qd - 1) % 2][:, b % 4, :], rhs, start=False,
                                                           stop=b % 10 == 9, skip_group_check=True)
                                mm.then_inc(r_ready, 1)
                                for b in range(CB):
                                    pe.wait_ge(hot_ready, cc * CB + b + 1)
                                    pe.matmul(ps[7][:, 0:WIN], ohq[b % RG][:], ohg[b % RG][:], start=False, stop=False,
                                              skip_group_check=True).then_inc(hot_used, 1)
                        pe.matmul(ps[7][:, 0:WIN], zero2[:, 0:P], zero2[:, 0:WIN], start=False, stop=True,
                                  skip_group_check=True).then_inc(win_done, 1)

                @block.vector
                def _(dve):
                    count = [0]

                    def step(ins):
                        ins.then_inc(dve2, 1)
                        count[0] += 1
                        dve.wait_ge(dve2, count[0])

                    windows = dve.value_load(nwin[0:1, 0:1], min_val=1, max_val=NW)
                    dve.sem_inc(lot_ready, 2)
                    dve.sem_inc(r_read, 1)
                    dve.sem_inc(hot_used, RG)
                    step(dve.memset(zscan[:], 0.0))
                    dve.memset(zero2[:], 0.0)
                    dve.memset(wshift[:], 0.0)
                    dve.tensor_copy(xpre[:, 0, :], nbase[:])
                    for h in range(NT):
                        dve.tensor_tensor_scan(xpre[:, 1:NB, h], hist[:, 0:NB - 1, h],
                                               zscan[:].broadcast_to([P, NB - 1]), nbase[:, h:h + 1],
                                               ALU.add, ALU.add)
                    dve.wait_ge(made2, 3)
                    step(dve.tensor_copy(gnum[:], gnum_i[:]))
                    dve.sem_inc(win_read, 1)
                    base = count[0]
                    QD = CB // 4
                    NSTEP = 6
                    with dve.Fori(0, windows) as w:
                        with dve.Fori(0, NC // 2) as j:
                            for i in range(2):
                                cc = w * NC + 2 * j + i
                                dve.wait_ge(lo_loaded[i], (w * (NC // 2) + j) * 16 + 16)
                                dve.tensor_scalar(xc[:], xpre[:, bass.ds((2 * j + i) * CB, CB), :]
                                                  .rearrange("p a b -> p (a b)"), wshift[:, 0:1], -256.0,
                                                  ALU.subtract, ALU.max).then_inc(dve2, 1)
                                dve.wait_ge(dve2, cc * 2 + base + 1)
                                dve.tensor_scalar(xw[i][:].rearrange("p a b -> p (a b)"), xc[:], 768.0, None,
                                                  ALU.min)
                                dve.tensor_scalar(lot[i][:].rearrange("p a b -> p (a b)"), lo_bc[i][:],
                                                  iota_p[:, 0:1], None, ALU.is_equal).then_inc(lot_ready, 1)
                                for qd in range(QD):
                                    dve.wait_ge(eq_ready, cc * QD + qd + 1)
                                    dve.tensor_tensor(eqm[qd % 2][:], ps[qd % 2][0:EB, 0:4 * EB]
                                                      .rearrange("p (a b) -> p a b", a=4),
                                                      earlier[:].unsqueeze(1).broadcast_to([EB, 4, EB]),
                                                      ALU.mult).then_inc(eq_masked, 1)
                                dve.wait_ge(r_ready, cc + 1)
                                for hb in range(2):
                                    c0 = bass.ds((2 * j + i) * CB + hb * (CB // 2), CB // 2)
                                    ins = dve.tensor_tensor(
                                        rm[hb][:], ps[2 + 2 * i + hb][0:EB, 0:CB * NT]
                                        .rearrange("p (a c b) -> p a c b", c=2, b=NT),
                                        oh_hi[:, c0, :].unsqueeze(2).broadcast_to([EB, CB // 2, 2, NT]), ALU.mult)
                                ins.then_inc(r_read, 1)
                                dve.wait_ge(r_read, cc + 2)
                                for hb in range(2):
                                    ins = dve.tensor_reduce(gq[i][:, hb * (CB // 2):(hb + 1) * (CB // 2), :], rm[hb][:],
                                                            AX_X, ALU.add)
                                ins.then_inc(dve2, 1)
                                dve.wait_ge(dve2, cc * 2 + base + 2)
                                for b in range(CB):
                                    dve.wait_ge(hot_used, cc * CB + b + 1)
                                    dve.tensor_scalar(ohq[b % RG][:], iota[0:EB, 0:P], gq[i][:, b, 1:2],
                                                      dv_e[:, bass.ds((2 * j + i) * CB + b, 1)], ALU.is_equal, ALU.mult)
                                    dve.tensor_scalar(ohg[b % RG][:], iota[0:EB, :], gq[i][:, b, 0:1], None,
                                                      ALU.is_equal).then_inc(hot_ready, 1)
                        dve.wait_ge(win_done, w + 1)
                        dve.tensor_scalar(tab_i[:], ps[7][:, 0:WIN], float(MID), None, ALU.add).then_inc(win_read, 1)
                        dve.tensor_tensor(tcmp[:], slotbase[0:WIN // 4, 1:NT].unsqueeze(1).broadcast_to([WIN // 4, 4, NT - 1]),
                                          gnum[:].unsqueeze(2).broadcast_to([WIN // 4, 4, NT - 1]),
                                          ALU.is_le).then_inc(table_chain, 1)
                        dve.wait_ge(table_chain, w * 2 + 1)
                        dve.tensor_reduce(tsum[:], tcmp[:], AX_X, ALU.add).then_inc(table_chain, 1)
                        dve.wait_ge(table_chain, w * 2 + 2)
                        dve.tensor_scalar(wshift[:], wshift[:], float(WIN), None, ALU.add)
                        dve.tensor_scalar(gnum[:], gnum[:], float(WIN), None, ALU.add)
                        dve.tensor_scalar(tof[:], tsum[:], float(D), None, ALU.mult).then_inc(table_made, 1)
                        dve.wait_ge(table_made, w + 1)
        c2.close()
        end_phase()

        c4 = ExitStack()
        ctx.callback(c4.close)

        def sb4(name, shape, dt=F32):
            return c4.enter_context(nc.sbuf_tensor(name, shape, dt))

        w_ab = sb4("w_ab", [P, LAYERS, H2, 2 * D])
        b_rows = sb4("b_rows", [P, NT, D])
        f_t = sb4("f_t", [P, H2, NP])
        xs = [sb4(f"xs{k}", [P, H2, P]) for k in range(U)]
        a_st = [sb4(f"a_st{k}", [P, D]) for k in range(U)]
        a_idx = [sb4(f"a_idx{k}", [P, 1], I32) for k in range(U)]
        bn_w = sb4("bn_w", [P, 2, LAYERS, H2])

        def tile_loop(eng, body, last=None):
            for k in range(U):
                body(0, k, False)
            with eng.Fori(1, NT // U - (last is not None)) as i:
                for k in range(U):
                    body(i, k, True)
            if last is not None:
                for k in range(U):
                    last(NT // U - 1, k)

        def flat(ap):
            return ap.rearrange("p a b -> p (a b)")

        class ProjectRows:

            def __init__(self, l):
                self.l = l
                self.in_ready, self.ab_ready, self.ab_read, self.a_staged, self.idx_ready = (
                    sem(f"{s}_{l}") for s in ("in_ready", "ab_ready", "ab_read", "a_staged", "idx_ready"))
                self.stored_before = 16 * (NT // U) * l
                self.a_stored = [gsem(f"a_stored{k}") for k in range(U)]

            def tensor(self, pe):
                def body(i, k, again):
                    pe.wait_ge(self.in_ready, i * U + k + 1)
                    if again:
                        pe.wait_ge(self.ab_read, (i - 1) * U + k + 1)
                    for h in range(H2):
                        mm = pe.matmul(ps[k][:], xs[k][:, h, :], w_ab[:, self.l, h, :], start=h == 0, stop=h == 1)
                    mm.then_inc(self.ab_ready, 1)
                tile_loop(pe, body)

            def vector(self, dve):
                def body(i, k, again):
                    dve.wait_ge(self.ab_ready, i * U + k + 1)
                    if again:
                        dve.wait_ge(self.a_stored[k], self.stored_before + i * 16)
                    dve.tensor_copy(a_st[k][:], ps[k][:, 0:D]).then_inc(self.a_staged, 1)
                    dve.tensor_copy(flat(b_rows[:, bass.ds(i * U + k, 1), :]), ps[k][:, D:2 * D]
                                    ).then_inc(self.ab_read, 1)
                tile_loop(dve, body)

            def gpsimd(self, pool):
                def body(i, k, again):
                    if again:
                        hold(pool, self.a_stored[k], self.stored_before + i * 16)
                    pool.tensor_copy(a_idx[k][:], rowid[:, bass.ds(i * U + k, 1)]).then_inc(self.idx_ready, 1)
                    hold(pool, self.idx_ready, i * U + k + 1)
                    hold(pool, self.a_staged, i * U + k + 1)
                    pool.indirect_dma_start(
                        a_rows[self.l], bass.IndirectOffsetOnAxis(ap=a_idx[k][:].bitcast(U32), axis=0),
                        a_st[k][:], None).then_inc(self.a_stored[k], 16)
                tile_loop(pool, body)
                for k in range(U):
                    pool.wait_ge(self.a_stored[k], self.stored_before + 16 * (NT // U))

        with ExitStack() as c5:
            def sb5(name, shape, dt=F32):
                return c5.enter_context(nc.sbuf_tensor(name, shape, dt))
            QC = 400
            NQ = NP // QC
            w_kv = sb5("w_kv", [P, H2, 2 * D])
            w_q = sb5("w_q", [P, H2, D])
            w_o = sb5("w_o", [P, H2, D])
            b_kv = sb5("b_kv", [P, 2 * D])
            b_q = sb5("b_q", [P, H2])
            b_o = sb5("b_o", [P, H2])
            q_t = sb5("q_t", [P, H2, NP])
            stats = sb5("stats", [P, NT, 6])
            mv = sb5("mv", [P, NT, 2])
            rstd = sb5("rstd", [P, NT])
            same = sb5("same", [P, P])
            kv_bd = sb5("kv_bd", [P, H2, P])
            ks_bd = sb5("ks_bd", [P, H2, P])
            zero3 = sb5("zero3", [P, 2 * (P + 1)])

            loaded3, x_loaded, neg_made, neg_stored = sem("loaded3"), sem("x_loaded"), sem("neg_made"), sem("neg_stored")
            w_sub, w_turned, w_copied = sem("w_sub"), sem("w_turned"), sem("w_copied")
            dve3, norm_ready, x_turned, x_copied = sem("dve3"), sem("norm_ready"), sem("x_turned"), sem("x_copied")
            var_ready, std_ready = sem("var_ready"), sem("std_ready")
            LOADS3 = 16 * (10 + 2 * LAYERS)

            with ExitStack() as c6:
                def sb6(name, shape, dt=F32):
                    return c6.enter_context(nc.sbuf_tensor(name, shape, dt))
                th = sb6("th", [P, LAYERS, H2, D])
                ph = sb6("ph", [P, LAYERS, H2, D])
                neg_row = sb6("neg_row", [1, D])
                xr = [sb6(f"xr{k}", [P, D]) for k in range(U)]
                id_f = sb6("id_f", [P, NT])
                id_g = sb6("id_g", [P, NT])

                with nc.Block() as block:
                    @block.sync
                    def _(sp):
                        sp.dma_start(xin[:], x_perm.rearrange("(h p) d -> p h d", p=P)).then_inc(x_loaded, 16)
                        r = "l (h p) i -> p l h i"
                        for l in range(LAYERS):
                            sp.dma_start(th[:, l], t["L0_gnn_thetas"][l].rearrange("(h p) i -> p h i", p=P)).then_inc(loaded3, 16)
                            sp.dma_start(ph[:, l], t["L0_gnn_phis"][l].rearrange("(h p) i -> p h i", p=P)).then_inc(loaded3, 16)
                        r = "(h p) o -> p h o"
                        sp.dma_start(w_kv[:, :, 0:D], t["L0_mix_wk"].rearrange(r, p=P)).then_inc(loaded3, 16)
                        sp.dma_start(w_kv[:, :, D:2 * D], t["L0_mix_wv"].rearrange(r, p=P)).then_inc(loaded3, 16)
                        sp.dma_start(w_q[:], t["L0_mix_wq"].rearrange(r, p=P)).then_inc(loaded3, 16)
                        sp.dma_start(w_o[:], t["L0_mix_wo"].rearrange(r, p=P)).then_inc(loaded3, 16)
                        sp.dma_start(b_kv[:, 0:D], t["L0_mix_bk"].partition_broadcast(P)).then_inc(loaded3, 16)
                        sp.dma_start(b_kv[:, D:2 * D], t["L0_mix_bv"].partition_broadcast(P)).then_inc(loaded3, 16)
                        r = "(h p) -> p h"
                        sp.dma_start(b_o[:], t["L0_mix_bo"].rearrange(r, p=P), allow_slow_non_contiguous=True
                                     ).then_inc(loaded3, 16)
                        sp.dma_start(b_q[:], t["L0_mix_bq"].rearrange(r, p=P), allow_slow_non_contiguous=True
                                     ).then_inc(loaded3, 16)
                        for i, name in enumerate(("L0_gnn_gammas", "L0_gnn_betas")):
                            sp.dma_start(bn_w[:, i], t[name].rearrange("l (h p) -> p l h", p=P),
                                         allow_slow_non_contiguous=True).then_inc(loaded3, 16)
                        sp.wait_ge(neg_made, 1)
                        for l in range(LAYERS):
                            sp.dma_start(a_rows[l][MID:MID + 1, :], neg_row[:]).then_inc(neg_stored, 16)
                        sp.wait_ge(neg_stored, 16 * LAYERS)
                        sp.wait_ge(loaded3, LOADS3)

                    @block.tensor
                    def _(pe):
                        pe.wait_ge(w_sub, 1)
                        for n in range(2 * LAYERS):
                            if n >= U:
                                pe.wait_ge(w_copied, n - U + 1)
                            w = (th, ph)[n % 2]
                            for ih in range(H2):
                                for oh in range(H2):
                                    mm = pe.transpose(ps[n % U][:, ih * D + oh * P:ih * D + (oh + 1) * P],
                                                      w[:, n // 2, oh, ih * P:(ih + 1) * P], ident[:])
                            mm.then_inc(w_turned, 1)
                        pe.wait_ge(w_copied, 2 * LAYERS)

                        def body(i, k, again):
                            pe.wait_ge(norm_ready, i * U + k + 1)
                            if again:
                                pe.wait_ge(x_copied, (i - 1) * U + k + 1)
                            for h in range(H2):
                                mm = pe.transpose(ps[k][:, h * P:(h + 1) * P], xr[k][:, h * P:(h + 1) * P], ident[:])
                            mm.then_inc(x_turned, 1)
                        tile_loop(pe, body)

                    @block.scalar
                    def _(act):
                        act.wait_ge(var_ready, 1)
                        act.activation(rstd[:], rstd[:], ACT.Sqrt).then_inc(std_ready, 1)
                        for n in range(2 * LAYERS):
                            act.wait_ge(w_turned, n + 1)
                            j = n % 2
                            act.copy(w_ab[:, n // 2, :, j * D:(j + 1) * D],
                                     ps[n % U][:].rearrange("p (h o) -> p h o", h=H2)).then_inc(w_copied, 1)

                        def body(i, k, again):
                            act.wait_ge(x_turned, i * U + k + 1)
                            act.copy(f_t[:, :, bass.ds((i * U + k) * P, P)],
                                     ps[k][:, 0:D].rearrange("p (h q) -> p h q", h=H2)).then_inc(x_copied, 1)
                        tile_loop(act, body)

                    @block.vector
                    def _(dve):
                        dve.memset(neg_row[:], NEG).then_inc(neg_made, 1)
                        dve.wait_ge(loaded3, LOADS3)
                        dve.tensor_tensor(ph[:], ph[:], th[:], ALU.subtract).then_inc(w_sub, 1)
                        dve.wait_ge(x_loaded, 16)
                        ids = xin[:, :, D:D + 1].bitcast(I32).rearrange("p t o -> p (t o)")
                        dve.tensor_copy(rowid[:], ids)
                        dve.tensor_copy(id_f[:], ids).then_inc(dve3, 1)
                        dve.wait_ge(dve3, 1)
                        dve.tensor_scalar(id_g[:], id_f[:], float(MID), None, ALU.is_gt).then_inc(dve3, 1)
                        for n in range(NT):
                            dve.bn_stats(stats[:, n, :], xin[:, n, 0:D])
                        dve.memset(zero3[:], 0.0).then_inc(dve3, 1)
                        dve.wait_ge(dve3, 3)
                        dve.tensor_tensor(nodeid[:], id_f[:], id_g[:], ALU.subtract)
                        for n in range(NT):
                            ins = dve.bn_aggr(mv[:, n, :], stats[:, n, :])
                        ins.then_inc(dve3, 1)
                        dve.wait_ge(dve3, 4)
                        dve.tensor_scalar(rstd[:], mv[:, :, 1], EPS, None, ALU.add).then_inc(var_ready, 1)
                        dve.memset(same[:], 0.0).then_inc(dve3, 1)
                        dve.wait_ge(dve3, 5)
                        dve.wait_ge(std_ready, 1)
                        dve.reciprocal(rstd[:], rstd[:]).then_inc(dve3, 1)
                        dve.wait_ge(dve3, 6)
                        for q in range(P // DH):
                            dve.memset(same[q * DH:(q + 1) * DH, q * DH:(q + 1) * DH], 1.0)

                        def body(i, k, again):
                            n = i * U + k
                            if again:
                                dve.wait_ge(x_turned, (i - 1) * U + k + 1)
                            dve.tensor_scalar(xr[k][:], flat(xin[:, bass.ds(n, 1), 0:D]),
                                              flat(mv[:, bass.ds(n, 1), 0:1]), rstd[:, bass.ds(n, 1)],
                                              ALU.subtract, ALU.mult).then_inc(norm_ready, 1)
                        tile_loop(dve, body)

            rows0 = ProjectRows(0)
            with nc.Block() as block:
                @block.scalar
                def _(act):
                    def body(i, k, again):
                        if again:
                            act.wait_ge(rows0.ab_ready, (i - 1) * U + k + 1)
                        act.copy(xs[k][:], f_t[:, :, bass.ds((i * U + k) * P, P)]).then_inc(rows0.in_ready, 1)
                    tile_loop(act, body)

                block.tensor(rows0.tensor)
                block.vector(rows0.vector)
                block.gpsimd(rows0.gpsimd)

            c7 = ExitStack()
            kb = [c7.enter_context(nc.sbuf_tensor(f"kb{k}", [P, 2 * D], F32)) for k in range(U)]
            ke = [c7.enter_context(nc.sbuf_tensor(f"ke{k}", [P, D], F32)) for k in range(U)]
            vf = [c7.enter_context(nc.sbuf_tensor(f"vf{k}", [P, H2, P + 1], F32)) for k in range(U)]
            in_ready3, kv_ready, kb_ready, k_neg, k_exp, k_done, kv_used = (
                sem(s) for s in ("in_ready3", "kv_ready", "kb_ready", "k_neg", "k_exp", "k_done", "kv_used"))
            kv_sum, ones_set, kv_masked = sem("kv_sum"), sem("ones_set"), sem("kv_masked")
            with nc.Block() as block:
                @block.gpsimd
                def _(pool):
                    for k in range(U):
                        pool.memset(vf[k][:, :, P:P + 1], 1.0).then_inc(ones_set, 1)

                @block.scalar
                def _(act):
                    def body(i, k, again):
                        if again:
                            act.wait_ge(kv_ready, (i - 1) * U + k + 1)
                        act.copy(xs[k][:], f_t[:, :, bass.ds((i * U + k) * P, P)]).then_inc(in_ready3, 1)
                        if k:
                            back(i, k - 1)

                    def back(i, k):
                        act.wait_ge(k_neg, i * U + k + 1)
                        act.activation(ke[k][:], ke[k][:], ACT.Exp).then_inc(k_exp, 1)
                        if k == U - 2:
                            act.wait_ge(k_neg, i * U + U)
                            act.activation(ke[U - 1][:], ke[U - 1][:], ACT.Exp).then_inc(k_exp, 1)
                    tile_loop(act, body)

                @block.tensor
                def _(pe):
                    pe.matmul(ps[7][:, 0:2 * (P + 1)], ident[:], zero3[:], start=True, stop=False,
                              skip_group_check=True)

                    def front(i, k, again):
                        pe.wait_ge(in_ready3, i * U + k + 1)
                        if again:
                            pe.wait_ge(kb_ready, (i - 1) * U + k + 1)
                        for h in range(H2):
                            mm = pe.matmul(ps[k][:], xs[k][:, h, :], w_kv[:, h, :], start=h == 0, stop=h == 1)
                        mm.then_inc(kv_ready, 1)

                    def back(i, k, rows):
                        pe.wait_ge(k_done, i * U + k + 1)
                        for g in range(H2):
                            mm = pe.matmul(ps[7][:, g * (P + 1):(g + 1) * (P + 1)], kb[k][0:rows, g * P:(g + 1) * P],
                                           vf[k][0:rows, g, :], start=False, stop=False, skip_group_check=True)
                        mm.then_inc(kv_used, 1)

                    def body(i, k, again):
                        front(i, k, again)
                        if k:
                            back(i, k - 1, P)
                        if k == U - 1:
                            back(i, k, P)

                    def last(i, k):
                        front(i, k, True)
                        if k:
                            back(i, k - 1, P)
                        if k == U - 1:
                            back(i, k, LAST)
                    pe.wait_ge(ones_set, U)
                    tile_loop(pe, body, last)
                    pe.matmul(ps[7][:, 0:2 * (P + 1)], ident[:], zero3[:], start=False, stop=True,
                              skip_group_check=True).then_inc(kv_sum, 1)

                @block.vector
                def _(dve):
                    def body(i, k, again):
                        n = i * U + k
                        dve.wait_ge(kv_ready, n + 1)
                        if again:
                            dve.wait_ge(kv_used, (i - 1) * U + k + 1)
                        dve.tensor_tensor(kb[k][:, 0:D], ps[k][:, 0:D], b_kv[:, 0:D], ALU.add)
                        dve.tensor_tensor(vf[k][:, :, 0:P], ps[k][:, D:2 * D].rearrange("p (g e) -> p g e", g=H2),
                                          b_kv[:, D:2 * D].rearrange("p (g e) -> p g e", g=H2), ALU.add
                                          ).then_inc(kb_ready, 1)
                        dve.wait_ge(kb_ready, n + 1)
                        dve.tensor_scalar(ke[k][:], kb[k][:, 0:D], 0.0, None, ALU.min).then_inc(k_neg, 1)
                        dve.wait_ge(k_exp, n + 1)
                        dve.scalar_tensor_tensor(kb[k][:, 0:D], kb[k][:, 0:D], 0.0, ke[k][:], ALU.max, ALU.add
                                                 ).then_inc(k_done, 1)
                    tile_loop(dve, body)
                    dve.wait_ge(kv_sum, 1)
                    for g in range(H2):
                        dve.tensor_tensor(kv_bd[:, g, :], same[:], ps[7][:, g * (P + 1):g * (P + 1) + P], ALU.mult)
                        dve.tensor_scalar(ks_bd[:, g, :], same[:], ps[7][:, g * (P + 1) + P:(g + 1) * (P + 1)], None,
                                          ALU.mult)
            c7.close()

            c8 = ExitStack()
            qe = [c8.enter_context(nc.sbuf_tensor(f"qe{k}", [P, QC], F32)) for k in range(2)]
            q_ready, q_read, q_neg, q_exp, q_done = (
                sem(s) for s in ("q_ready", "q_read", "q_neg", "q_exp", "q_done"))
            nd_ready, den_set, quot_ready, o_ready, o_read = (
                sem(s) for s in ("nd_ready", "den_set", "quot_ready", "o_ready", "o_read"))
            with nc.Block() as block:
                def chunk_loop(eng, body):
                    for o in range(H2):
                        body(0, o, False)
                    with eng.Fori(1, NQ) as i:
                        for o in range(H2):
                            body(i, o, True)

                @block.tensor
                def _(pe):
                    def q_body(i, o, again):
                        if again:
                            pe.wait_ge(q_read, (i - 1) * H2 + o + 1)
                        for h in range(H2):
                            mm = pe.matmul(ps[o][:, 0:QC], w_q[:, h, o * P:(o + 1) * P],
                                           f_t[:, h, bass.ds(i * QC, QC)], start=h == 0, stop=h == 1)
                        mm.then_inc(q_ready, 1)
                    chunk_loop(pe, q_body)

                    def nd_body(i, g, again):
                        pe.wait_ge(q_done, i * H2 + g + 1)
                        if again:
                            pe.wait_ge(quot_ready, (i - 1) * H2 + g + 1)
                        col = bass.ds(i * QC, QC)
                        pe.matmul(ps[2 + 2 * g][:, 0:QC], kv_bd[:, g, :], q_t[:, g, col])
                        pe.matmul(ps[3 + 2 * g][:, 0:QC], ks_bd[:, g, :], q_t[:, g, col]).then_inc(nd_ready, 1)
                    chunk_loop(pe, nd_body)

                    def o_body(i, o, again):
                        pe.wait_ge(quot_ready, i * H2 + 2)
                        if again:
                            pe.wait_ge(o_read, (i - 1) * H2 + o + 1)
                        for g in range(H2):
                            mm = pe.matmul(ps[6 + o][:, 0:QC], w_o[:, g, o * P:(o + 1) * P],
                                           q_t[:, g, bass.ds(i * QC, QC)], start=g == 0, stop=g == 1)
                        mm.then_inc(o_ready, 1)
                    chunk_loop(pe, o_body)

                @block.scalar
                def _(act):
                    def q_body(i, o, again):
                        n = i * H2 + o
                        act.wait_ge(q_neg, n + 1)
                        act.activation(q_t[:, o, bass.ds(i * QC, QC)], ps[o][:, 0:QC], ACT.Relu,
                                       bias=b_q[:, o:o + 1]).then_inc(q_read, 1)
                        act.activation(qe[o][:], qe[o][:], ACT.Exp).then_inc(q_exp, 1)
                    chunk_loop(act, q_body)

                    def o_body(i, o, again):
                        act.wait_ge(o_ready, i * H2 + o + 1)
                        act.activation(f_t[:, o, bass.ds(i * QC, QC)], ps[6 + o][:, 0:QC], ACT.Identity,
                                       bias=b_o[:, o:o + 1]).then_inc(o_read, 1)
                    chunk_loop(act, o_body)

                @block.vector
                def _(dve):
                    def q_body(i, o, again):
                        n = i * H2 + o
                        dve.wait_ge(q_ready, n + 1)
                        dve.tensor_scalar(qe[o][:], ps[o][:, 0:QC], b_q[:, o:o + 1], 0.0, ALU.add, ALU.min
                                          ).then_inc(q_neg, 1)
                        dve.wait_ge(q_exp, n + 1)
                        col = q_t[:, o, bass.ds(i * QC, QC)]
                        dve.tensor_tensor(col, col, qe[o][:], ALU.add).then_inc(q_done, 1)
                    chunk_loop(dve, q_body)

                    def nd_body(i, g, again):
                        n = i * H2 + g
                        dve.wait_ge(nd_ready, n + 1)
                        dve.tensor_scalar(qe[g][:], ps[3 + 2 * g][:, 0:QC], 1e-6, None, ALU.add).then_inc(den_set, 1)
                        dve.wait_ge(den_set, 2 * n + 1)
                        dve.reciprocal(qe[g][:], qe[g][:]).then_inc(den_set, 1)
                        dve.wait_ge(den_set, 2 * n + 2)
                        dve.tensor_tensor(q_t[:, g, bass.ds(i * QC, QC)], ps[2 + 2 * g][:, 0:QC], qe[g][:], ALU.mult
                                          ).then_inc(quot_ready, 1)
                    chunk_loop(dve, nd_body)
            c8.close()

        end_phase()

        ring = [sb4(f"ring{k}", [P, D]) for k in range(K)]
        slot_idx = [sb4(f"slot_idx{h}", [P, K // 2], I32) for h in range(2)]
        tab = sb4("tab", [P, WIN], I32)
        tiles_of = sb4("tiles_of", [1, WIN], I32)
        best = sb4("best", [P, NT * D])
        agg_t = sb4("agg_t", [P, H2, NP])
        st = [sb4(f"st{k}", [P, D]) for k in range(U)]
        HK = K // 2
        for l in range(LAYERS):
            best_set, tab_loaded, idx_set, used, win_over = (
                sem(f"{s}_{l}") for s in ("best_set", "tab_loaded", "idx_set", "used", "win_over"))
            landed = [gsem(f"landed{k}_{l}") for k in range(K)]
            with nc.Block() as block:
                @block.sync
                def _(sp):
                    windows = sp.value_load(nwin[0:1, 0:1], min_val=1, max_val=NW)
                    with sp.Fori(0, windows) as w:
                        hold(sp, win_over, w + 1)
                        sp.dma_start(tab[:], table_dram[bass.ds(w, 1)].rearrange("o p g -> (o p) g")
                                     ).then_inc(tab_loaded, 16)
                        sp.dma_start(tiles_of[:], tile_dram[bass.ds(w, 1)]).then_inc(tab_loaded, 16)

                @block.gpsimd
                def _(pool):
                    windows = pool.value_load(nwin[0:1, 0:1], min_val=1, max_val=NW)
                    with pool.Fori(0, windows) as w:
                        hold(pool, tab_loaded, w * 32 + 32)
                        steps = pool.value_load(nstep[0:1, bass.ds(w, 1)], min_val=1, max_val=WIN // K)
                        with pool.Fori(0, steps) as c:
                            gc = w * (WIN // K) + c
                            for h in range(2):
                                hold(pool, used, gc * K + (h + 1) * HK)
                                pool.tensor_copy(slot_idx[h][:], tab[:, bass.ds(c * K + h * HK, HK)]
                                                 ).then_inc(idx_set, 1)
                                hold(pool, idx_set, gc * 2 + h + 1)
                                for k in range(HK):
                                    pool.indirect_dma_start(
                                        ring[h * HK + k][:], None, a_rows[l],
                                        bass.IndirectOffsetOnAxis(ap=slot_idx[h][:, k:k + 1].bitcast(U32), axis=0)
                                    ).then_inc(landed[h * HK + k], 16)

                @block.vector
                def _(dve):
                    windows = dve.value_load(nwin[0:1, 0:1], min_val=1, max_val=NW)
                    dve.memset(best[:], NEG).then_inc(used, K)
                    dve.sem_inc(win_over, 1)
                    dve.wait_ge(used, K)
                    with dve.Fori(0, windows) as w:
                        dve.wait_ge(tab_loaded, w * 32 + 32)
                        steps = dve.value_load(nstep[0:1, bass.ds(w, 1)], min_val=1, max_val=WIN // K)
                        with dve.Fori(0, steps) as c:
                            gc = w * (WIN // K) + c
                            _, offs = nc.values_load_multi_w_load_instructions(
                                tiles_of[0:1, bass.ds(c * K, K)], engines=[mybir.EngineType.DVE],
                                min_val=0, max_val=(NT - 1) * D)
                            for k in range(K):
                                m = best[:, bass.ds(offs[k], D)]
                                dve.wait_ge(landed[k], gc * 16 + 16)
                                dve.wait_ge(used, gc * K + K + k)
                                dve.tensor_tensor(m, m, ring[k][:], ALU.max).then_inc(used, 1)
                        dve.sem_inc(win_over, 1)

            sum_ready, sum_turned, agg_copied, dve5 = (
                sem(f"{s}_{l}") for s in ("sum_ready", "sum_turned", "agg_copied", "dve5"))
            bn_ready, bvar_ready, bstd_ready = (sem(f"{s}_{l}") for s in ("bn_ready", "bvar_ready", "bstd_ready"))
            bstats = sb4(f"bstats_{l}", [P, H2, 7, 6])
            bmv = sb4(f"bmv_{l}", [P, H2, 2])
            scale = sb4(f"scale_{l}", [P, H2])
            shift = sb4(f"shift_{l}", [P, H2])
            rows = ProjectRows(l + 1) if l + 1 < LAYERS else None
            if rows is None:
                y_ready, y_turned, y_added = sem("y_ready"), sem("y_turned"), sem("y_added")
                out_ready = sem("out_ready")
            with nc.Block() as block:
                @block.tensor
                def _(pe):
                    def body(i, k, again):
                        pe.wait_ge(sum_ready, i * U + k + 1)
                        if again:
                            pe.wait_ge(agg_copied, (i - 1) * U + k + 1)
                        for h in range(H2):
                            mm = pe.transpose(ps[k][:, h * P:(h + 1) * P], st[k][:, h * P:(h + 1) * P], ident[:])
                        mm.then_inc(sum_turned, 1)
                    tile_loop(pe, body)
                    pe.wait_ge(agg_copied, NT)
                    if rows:
                        rows.tensor(pe)
                    else:
                        def body(i, k, again):
                            pe.wait_ge(out_ready, i * U + k + 1)
                            if again:
                                pe.wait_ge(y_added, (i - 1) * U + k + 1)
                            for h in range(H2):
                                mm = pe.transpose(ps[k][:, h * P:(h + 1) * P], xs[k][:, h, :], ident[:])
                            mm.then_inc(y_turned, 1)
                        tile_loop(pe, body)

                @block.scalar
                def _(act):
                    def body(i, k, again):
                        act.wait_ge(sum_turned, i * U + k + 1)
                        act.activation(agg_t[:, :, bass.ds((i * U + k) * P, P)],
                                       ps[k][:, 0:D].rearrange("p (h q) -> p h q", h=H2), ACT.Relu
                                       ).then_inc(agg_copied, 1)
                    tile_loop(act, body)
                    act.wait_ge(bvar_ready, 1)
                    act.activation(scale[:], scale[:], ACT.Sqrt).then_inc(bstd_ready, 1)
                    act.wait_ge(bn_ready, 1)

                    def body(i, k, again):
                        if again:
                            act.wait_ge(rows.ab_ready if rows else y_turned, (i - 1) * U + k + 1)
                        for h in range(H2):
                            ins = act.activation(xs[k][:, h, :], agg_t[:, h, bass.ds((i * U + k) * P, P)], ACT.Relu,
                                                 bias=shift[:, h:h + 1], scale=scale[:, h:h + 1])
                        ins.then_inc(rows.in_ready if rows else y_ready, 1)
                    tile_loop(act, body)

                @block.vector
                def _(dve):
                    def body(i, k, again):
                        if again:
                            dve.wait_ge(sum_turned, (i - 1) * U + k + 1)
                        n = i * U + k
                        dve.tensor_tensor(st[k][:], best[:, bass.ds(n * D, D)], flat(b_rows[:, bass.ds(n, 1), :]),
                                          ALU.add).then_inc(sum_ready, 1)
                    tile_loop(dve, body)
                    dve.wait_ge(agg_copied, NT)
                    count = [0]

                    def step(ins):
                        ins.then_inc(dve5, 1)
                        count[0] += 1
                        dve.wait_ge(dve5, count[0])
                    for h in range(H2):
                        for j in range(7):
                            ins = dve.bn_stats(bstats[:, h, j, :], agg_t[:, h, j * 512:min(j * 512 + 512, N)])
                    step(ins)
                    for h in range(H2):
                        ins = dve.bn_aggr(bmv[:, h, :], flat(bstats[:, h]))
                    step(ins)
                    dve.tensor_scalar(scale[:], bmv[:, :, 1], EPS, None, ALU.add).then_inc(bvar_ready, 1)
                    dve.wait_ge(bstd_ready, 1)
                    step(dve.reciprocal(scale[:], scale[:]))
                    step(dve.tensor_tensor(scale[:], scale[:], bn_w[:, 0, l, :], ALU.mult))
                    step(dve.tensor_tensor(shift[:], bmv[:, :, 0], scale[:], ALU.mult))
                    dve.tensor_tensor(shift[:], bn_w[:, 1, l, :], shift[:], ALU.subtract).then_inc(bn_ready, 1)
                    if rows:
                        rows.vector(dve)
                    else:
                        def body(i, k, again):
                            n = i * U + k
                            dve.wait_ge(y_ready, n + 1)
                            dve.tensor_tensor(xs[k][:], xs[k][:], f_t[:, :, bass.ds(n * P, P)], ALU.add
                                              ).then_inc(out_ready, 1)
                            if k:
                                add(i, k - 1)
                            if k == U - 1:
                                add(i, k)

                        def add(i, k):
                            n = i * U + k
                            dve.wait_ge(y_turned, n + 1)
                            m = flat(xin[:, bass.ds(n, 1), 0:D])
                            dve.tensor_tensor(m, m, ps[k][:, 0:D], ALU.add).then_inc(y_added, 1)
                        tile_loop(dve, body)

                if rows:
                    block.gpsimd(rows.gpsimd)
            end_phase()
        c4.close()

        ET = (2 * N) // P + EXPERTS
        c9 = ExitStack()
        ctx.callback(c9.close)

        def sb9(name, shape, dt=F32):
            return c9.enter_context(nc.sbuf_tensor(name, shape, dt))

        HC = HID // P
        w1 = sb9("w1", [P, EXPERTS, H2, HID])
        w2 = sb9("w2", [P, EXPERTS, HC, D])
        b1 = sb9("b1", [P, EXPERTS, HID])
        b2 = sb9("b2", [P, EXPERTS, D])
        place = [sb9(f"place{i}", [P, NT], I32) for i in range(2)]
        weight = sb9("weight", [P, 2, NT])
        expert_of = sb9("expert_of", [1, 64], I32)
        npairs = sb9("npairs", [1, 1], I32)
        w_loaded, routed, y_stored_all = sem("w_loaded"), sem("routed"), sem("y_stored_all")
        xb_dram = dram("xb_dram", ((ET + 2) * P, D))
        y_dram = dram("y_dram", ((ET + 2) * P, D))
        with ExitStack() as c10:
            def sb10(name, shape, dt=F32):
                return c10.enter_context(nc.sbuf_tensor(name, shape, dt))
            xb = sb10("xb", [P, NT, D])
            w_r = sb10("w_r", [P, H2, EXPERTS])
            b_r = sb10("b_r", [P, EXPERTS])
            gam = sb10("gam", [P, D])
            bet = sb10("bet", [P, D])
            zrow = sb10("zrow", [P, D])
            stats5 = sb10("stats5", [P, 2, NT, 6])
            mv5 = sb10("mv5", [P, 2, NT, 2])
            rstd5 = sb10("rstd5", [P, 2, NT])
            xt5 = [sb10(f"xt5_{k}", [P, H2, P]) for k in range(U)]
            xrow5 = [sb10(f"xrow5_{k}", [P, D]) for k in range(U)]
            logit = sb10("logit", [P, NT, EXPERTS])
            oh = [sb10(f"oh{i}", [P, NT, EXPERTS]) for i in range(2)]
            work = sb10("work", [P, NT, EXPERTS])
            top = [sb10(f"top{i}", [P, NT]) for i in range(2)]
            which = sb10("which", [P, NT])
            valid = sb10("valid", [P, 1])
            before = sb10("before", [P, P])
            ones = sb10("ones", [P, P])
            both = sb10("both", [P, NT, EXPERTS])
            prefix = sb10("prefix", [P, NT + 1, EXPERTS])
            cnt_i = sb10("cnt_i", [P, 2, EXPERTS], I32)
            tiles_f = sb10("tiles_f", [P, EXPERTS])
            tbase = sb10("tbase", [P, EXPERTS + 1])
            place_f = sb10("place_f", [P, NT])
            jcmp = sb10("jcmp", [1, 64, EXPERTS - 1])
            jsum = sb10("jsum", [1, 64])
            jp = sb10("jp", [1, 2])
            jp_i = sb10("jp_i", [1, 2], I32)
            iota_e = sb10("iota_e", [P, EXPERTS])
            iota_j = sb10("iota_j", [1, 64])

            made5, dve5, small_loaded, zero_stored = sem("made5"), sem("dve5x"), sem("small_loaded"), sem("zero_stored")
            var_ready, std_ready, xb_ready, xb_turned, xt_ready, logit_ready, logit_read = (
                sem(s) for s in ("var_ready5", "std_ready5", "xb_ready", "xb_turned", "xt_ready", "logit_ready",
                                 "logit_read"))
            both_ready, counted, diff_ready, exp_ready, placed, sent = (
                (gsem if s == "sent" else sem)(s)
                for s in ("both_ready", "counted", "diff_ready", "exp_ready", "placed", "sent"))
            with nc.Block() as block:
                @block.sync
                def _(sp):
                    sp.dma_start(w_r[:], t["L0_ffn_Wr"].rearrange("(h p) e -> p h e", p=P)).then_inc(small_loaded, 16)
                    sp.dma_start(b_r[:], t["L0_ffn_br"].partition_broadcast(P)).then_inc(small_loaded, 16)
                    sp.dma_start(gam[:], t["L0_ffn_gamma"].partition_broadcast(P)).then_inc(small_loaded, 16)
                    sp.dma_start(bet[:], t["L0_ffn_beta"].partition_broadcast(P)).then_inc(small_loaded, 16)
                    sp.wait_ge(made5, 1)
                    for j in range(0, ET + 2, NT):
                        m = min(NT, ET + 2 - j)
                        sp.dma_start(xb_dram[j * P:(j + m) * P, :].rearrange("(p a) d -> p a d", a=m),
                                     zrow[:].unsqueeze(1).broadcast_to([P, m, D])).then_inc(zero_stored, 16)
                    full = 2 * N // P
                    m = ET + 2 - full
                    sp.dma_start(y_dram[full * P:(ET + 2) * P, :].rearrange("(p a) d -> p a d", a=m),
                                 zrow[:].unsqueeze(1).broadcast_to([P, m, D])).then_inc(zero_stored, 16)
                    for e in range(EXPERTS):
                        sp.dma_start(w1[:, e], t["L0_ffn_W1"][e].rearrange("(h p) o -> p h o", p=P)).then_inc(w_loaded, 16)
                        sp.dma_start(w2[:, e], t["L0_ffn_W2"][e].rearrange("(h p) o -> p h o", p=P)).then_inc(w_loaded, 16)
                    sp.dma_start(flat(b1[:]), t["L0_ffn_b1"].rearrange("e o -> (e o)").partition_broadcast(P)
                                 ).then_inc(w_loaded, 16)
                    sp.dma_start(flat(b2[:]), t["L0_ffn_b2"].rearrange("e o -> (e o)").partition_broadcast(P)
                                 ).then_inc(w_loaded, 16)
                    sp.wait_ge(w_loaded, 16 * (2 * EXPERTS + 2))
                    sp.wait_ge(zero_stored, 16 * (-(-(ET + 2) // NT) + 1))
                    sp.wait_ge(sent, 16 * 2 * NT)

                @block.gpsimd
                def _(pool):
                    pool.memset(zrow[:], 0.0).then_inc(made5, 1)
                    pool.memset(before[:], 1.0).then_inc(made5, 1)
                    pool.wait_ge(made5, 2)
                    pool.affine_select(out=before[:], in_=before[:], compare_op=ALU.is_gt, fill=0.0, base=0,
                                       pattern=[[1, P]], channel_multiplier=-1).then_inc(made5, 1)
                    pool.memset(ones[:], 1.0).then_inc(made5, 1)
                    pool.iota(iota_e[:], [[1, EXPERTS]], base=0, channel_multiplier=0,
                              allow_small_or_imprecise_dtypes=True).then_inc(made5, 1)
                    pool.iota(iota_j[:], [[1, 64]], base=0, channel_multiplier=0,
                              allow_small_or_imprecise_dtypes=True).then_inc(made5, 1)
                    pool.wait_ge(zero_stored, 16 * (-(-(ET + 2) // NT) + 1))
                    pool.wait_ge(placed, 2)
                    for n in range(NT):
                        r = P if n < NT - 1 else LAST
                        for i in range(2):
                            pool.indirect_dma_start(
                                xb_dram, bass.IndirectOffsetOnAxis(ap=place[i][0:r, n:n + 1].bitcast(U32), axis=0),
                                xb[0:r, n, :], None).then_inc(sent, 16)

                @block.tensor
                def _(pe):
                    pe.wait_ge(small_loaded, 64)

                    def front(i, k, again):
                        pe.wait_ge(xb_ready, i * U + k + 1)
                        if again:
                            pe.wait_ge(xt_ready, (i - 1) * U + k + 1)
                        for h in range(H2):
                            mm = pe.transpose(ps[k][:, h * P:(h + 1) * P], xrow5[k][:, h * P:(h + 1) * P],
                                              ident[:])
                        mm.then_inc(xb_turned, 1)

                    def body(i, k, again):
                        front(i, k, again)
                        if k:
                            back(i, k - 1, again)
                        if k == U - 1:
                            back(i, k, again)

                    def back(i, k, again):
                        pe.wait_ge(xt_ready, i * U + k + 1)
                        if again:
                            pe.wait_ge(logit_read, (i - 1) * U + k + 1)
                        for h in range(H2):
                            mm = pe.matmul(ps[k][:, D:D + EXPERTS], xt5[k][:, h, :], w_r[:, h, :], start=h == 0,
                                           stop=h == 1)
                        mm.then_inc(logit_ready, 1)
                    tile_loop(pe, body)
                    pe.wait_ge(made5, 6)
                    pe.wait_ge(both_ready, 1)
                    pe.matmul(ps[5][:, 0:NT * EXPERTS], before[:], flat(both[:]))
                    pe.matmul(ps[6][:, 0:NT * EXPERTS], ones[:], flat(both[:])).then_inc(counted, 1)

                @block.scalar
                def _(act):
                    for i in range(2):
                        act.wait_ge(var_ready, i + 1)
                        act.activation(rstd5[:, i, :], rstd5[:, i, :], ACT.Sqrt).then_inc(std_ready, 1)

                    def body(i, k, again):
                        n = i * U + k
                        act.wait_ge(xb_turned, n + 1)
                        if again:
                            act.wait_ge(logit_ready, (i - 1) * U + k + 1)
                        act.copy(flat(xt5[k][:]), ps[k][:, 0:D]).then_inc(xt_ready, 1)
                    tile_loop(act, body)
                    act.wait_ge(diff_ready, 1)
                    act.activation(weight[:, 1, :], weight[:, 0, :], ACT.Exp).then_inc(exp_ready, 1)

                @block.vector
                def _(dve):
                    count = [0]

                    def step(ins):
                        ins.then_inc(dve5, 1)
                        count[0] += 1
                        dve.wait_ge(dve5, count[0])
                    dve.wait_ge(small_loaded, 64)
                    for m in range(2):
                        x_in = (xin, xb)[m]
                        for n in range(NT):
                            ins = dve.bn_stats(stats5[:, m, n, :], x_in[:, n, 0:D])
                        step(ins)
                        for n in range(NT):
                            ins = dve.bn_aggr(mv5[:, m, n, :], stats5[:, m, n, :])
                        step(ins)
                        dve.tensor_scalar(rstd5[:, m, :], mv5[:, m, :, 1], EPS, None, ALU.add).then_inc(var_ready, 1)
                        dve.wait_ge(std_ready, m + 1)
                        step(dve.reciprocal(rstd5[:, m, :], rstd5[:, m, :]))
                        for n in range(NT):
                            ins = dve.tensor_scalar(xb[:, n, :], x_in[:, n, 0:D], mv5[:, m, n, 0:1],
                                                    rstd5[:, m, n:n + 1], ALU.subtract, ALU.mult)
                        step(ins)
                    rows3 = [P, NT, D]
                    step(dve.tensor_tensor(xb[:], xb[:], gam[:].unsqueeze(1).broadcast_to(rows3), ALU.mult))
                    step(dve.tensor_tensor(xb[:], xb[:], bet[:].unsqueeze(1).broadcast_to(rows3), ALU.add))

                    def body(i, k, again):
                        n = i * U + k
                        if again:
                            dve.wait_ge(xb_turned, (i - 1) * U + k + 1)
                        dve.tensor_copy(xrow5[k][:], flat(xb[:, bass.ds(n, 1), :])).then_inc(xb_ready, 1)
                        if k:
                            read(i, k - 1)
                        if k == U - 1:
                            read(i, k)

                    def read(i, k):
                        n = i * U + k
                        dve.wait_ge(logit_ready, n + 1)
                        dve.tensor_tensor(flat(logit[:, bass.ds(n, 1), :]), ps[k][:, D:D + EXPERTS], b_r[:], ALU.add
                                          ).then_inc(logit_read, 1)
                    tile_loop(dve, body)
                    dve.wait_ge(logit_read, NT)
                    dve.wait_ge(made5, 6)
                    sh = [P, NT, EXPERTS]
                    e_bc = iota_e[:].unsqueeze(1).broadcast_to(sh)
                    for i in range(2):
                        step(dve.tensor_reduce(top[i][:], logit[:], AX_X, ALU.max))
                        step(dve.tensor_tensor(work[:], logit[:], top[i][:].unsqueeze(2).broadcast_to(sh), ALU.is_lt))
                        step(dve.scalar_tensor_tensor(work[:], work[:], float(EXPERTS), e_bc, ALU.mult, ALU.add))
                        step(dve.tensor_reduce(which[:], work[:], AX_X, ALU.min))
                        step(dve.tensor_tensor(oh[i][:], e_bc, which[:].unsqueeze(2).broadcast_to(sh), ALU.is_equal))
                        if i == 0:
                            step(dve.scalar_tensor_tensor(logit[:], oh[0][:], NEG, logit[:], ALU.mult, ALU.add))
                    step(dve.tensor_scalar(valid[:], iota_p[:], float(LAST), None, ALU.is_lt))
                    for i in range(2):
                        step(dve.tensor_scalar(oh[i][:, NT - 1, :], oh[i][:, NT - 1, :], valid[:, 0:1], None, ALU.mult))
                    dve.tensor_tensor(weight[:, 0, :], top[1][:], top[0][:], ALU.subtract).then_inc(diff_ready, 1)
                    dve.tensor_tensor(both[:], oh[0][:], oh[1][:], ALU.add).then_inc(both_ready, 1)
                    dve.wait_ge(exp_ready, 1)
                    step(dve.tensor_scalar(weight[:, 0, :], weight[:, 1, :], 1.0, None, ALU.add))
                    step(dve.reciprocal(weight[:, 0, :], weight[:, 0, :]))
                    step(dve.tensor_tensor(weight[:, 1, :], weight[:, 1, :], weight[:, 0, :], ALU.mult))
                    dve.wait_ge(counted, 1)
                    step(dve.memset(prefix[:], 0.0))
                    step(dve.tensor_copy(work[:], ps[6][:, 0:NT * EXPERTS].rearrange("p (a b) -> p a b", b=EXPERTS)))
                    zcol = prefix[:, 0:1, 0:1].rearrange("p a b -> p (a b)").broadcast_to([P, NT])
                    for e in range(EXPERTS):
                        ins = dve.tensor_tensor_scan(prefix[:, 1:NT + 1, e], work[:, :, e], zcol, 0.0, ALU.add, ALU.add)
                    step(ins)
                    step(dve.tensor_scalar(tiles_f[:], prefix[:, NT, :], float(P - 1), None, ALU.add))
                    step(dve.tensor_copy(cnt_i[:, 0, :], tiles_f[:]))
                    step(dve.tensor_scalar(cnt_i[:, 1, :], cnt_i[:, 0, :], 7, None, ALU.logical_shift_right))
                    step(dve.tensor_copy(tiles_f[:], cnt_i[:, 1, :]))
                    step(dve.memset(tbase[:], 0.0))
                    step(dve.tensor_tensor_scan(tbase[:, 1:EXPERTS + 1], tiles_f[:], zcol[:, 0:EXPERTS], 0.0, ALU.add, ALU.add))
                    step(dve.scalar_tensor_tensor(work[:], tbase[:, 0:EXPERTS].unsqueeze(1).broadcast_to(sh), float(P),
                                                  prefix[:, 0:NT, :], ALU.mult, ALU.add))
                    step(dve.tensor_tensor(work[:], work[:], ps[5][:, 0:NT * EXPERTS].rearrange(
                        "p (a b) -> p a b", b=EXPERTS), ALU.add))
                    for i in range(2):
                        step(dve.tensor_tensor(oh[i][:], oh[i][:], work[:], ALU.mult))
                        step(dve.tensor_reduce(place_f[:], oh[i][:], AX_X, ALU.add))
                        step(dve.tensor_copy(place[i][:], place_f[:]))
                        dve.sem_inc(placed, 1)
                    shj = [1, 64, EXPERTS - 1]
                    step(dve.tensor_tensor(jcmp[:], tbase[0:1, 1:EXPERTS].unsqueeze(1).broadcast_to(shj),
                                           iota_j[:].unsqueeze(2).broadcast_to(shj), ALU.is_le))
                    step(dve.tensor_reduce(jsum[:], jcmp[:], AX_X, ALU.add))
                    step(dve.tensor_copy(expert_of[:], jsum[:]))
                    step(dve.tensor_scalar(jp[:, 0:1], tbase[0:1, EXPERTS:EXPERTS + 1], 1.0, None, ALU.add))
                    step(dve.tensor_copy(jp_i[:, 0:1], jp[:, 0:1]))
                    step(dve.tensor_scalar(npairs[:], jp_i[:, 0:1], 1, None, ALU.logical_shift_right))

        with ExitStack() as c11:
            def ring2(name, shape):
                return [c11.enter_context(nc.sbuf_tensor(f"{name}{k}", shape, F32)) for k in range(2)]
            row5 = ring2("row5_", [P, D])
            xt = ring2("xt", [P, H2, P])
            hb = ring2("hb", [P, HID])
            hg = ring2("hg", [P, HID])
            ht = ring2("ht", [P, HC, P])
            yo = ring2("yo", [P, D])
            row_loaded = [sem(f"row_loaded{k}") for k in range(2)]
            y_stored = [sem(f"y_stored{k}") for k in range(2)]
            xt_turned, xt_ready, h_ready, h_biased, h_done, h_turned, ht_ready, y_ready, y_biased = (
                sem(s) for s in ("xt_turned6", "xt_ready6", "h_ready", "h_biased", "h_done", "h_turned", "ht_ready",
                                 "y_ready6", "y_biased"))

            def past(eng, semaphore, value):
                if not isinstance(value, int) or value > 0:
                    eng.wait_ge(semaphore, value)

            def expert(eng, j):
                return eng.value_load(expert_of[0:1, bass.ds(j, 1)], min_val=0, max_val=EXPERTS - 1)

            def pair_loop(eng, step):
                pairs = eng.value_load(npairs[0:1, 0:1], min_val=2, max_val=ET // 2)
                for j in range(2):
                    step(j, j)
                with eng.Fori(1, pairs) as c:
                    for k in range(2):
                        step(2 * c + k, k)

            with nc.Block() as block:
                @block.sync
                def _(sp):
                    def load(j, k):
                        if not isinstance(j, int) or j >= 2:
                            hold(sp, xt_turned, j - 1)
                        sp.dma_start(row5[k][:], xb_dram[bass.ds(j * P, P), :]).then_inc(row_loaded[k], 16)

                    def step(j, k):
                        load(j + 2, k)
                        hold(sp, y_biased, j + 1)
                        sp.dma_start(y_dram[bass.ds(j * P, P), :], yo[k][:]).then_inc(y_stored[k], 16)
                    load(0, 0)
                    load(1, 1)
                    pair_loop(sp, step)
                    pairs = sp.value_load(npairs[0:1, 0:1], min_val=2, max_val=ET // 2)
                    for k in range(2):
                        hold(sp, y_stored[k], pairs * 16)

                @block.tensor
                def _(pe):
                    def turn_x(j, k):
                        pe.wait_ge(row_loaded[k], (j - k) * 8 + 16)
                        past(pe, xt_ready, j - 1)
                        for h in range(H2):
                            mm = pe.transpose(ps[k][:, h * P:(h + 1) * P], row5[k][:, h * P:(h + 1) * P], ident[:])
                        mm.then_inc(xt_turned, 1)

                    def hidden(j, k, e):
                        pe.wait_ge(xt_ready, j + 1)
                        past(pe, h_biased, j - 1)
                        for h in range(H2):
                            mm = pe.matmul(ps[2 + k][:], xt[k][:, h, :],
                                           w1[:, bass.ds(e, 1), h, :].rearrange("p a o -> p (a o)"),
                                           start=h == 0, stop=h == 1)
                        mm.then_inc(h_ready, 1)

                    def step(j, k):
                        e_next, e = expert(pe, j + 1), expert(pe, j)
                        hidden(j + 1, 1 - k, e_next)
                        pe.wait_ge(h_done, j + 1)
                        past(pe, ht_ready, j - 1)
                        for h in range(HC):
                            mm = pe.transpose(ps[4 + k][:, h * P:(h + 1) * P], hg[k][:, h * P:(h + 1) * P], ident[:])
                        mm.then_inc(h_turned, 1)
                        turn_x(j + 2, k)
                        pe.wait_ge(ht_ready, j + 1)
                        past(pe, y_biased, j - 1)
                        for h in range(HC):
                            mm = pe.matmul(ps[6 + k][:, 0:D], ht[k][:, h, :],
                                           w2[:, bass.ds(e, 1), h, :].rearrange("p a o -> p (a o)"),
                                           start=h == 0, stop=h == HC - 1)
                        mm.then_inc(y_ready, 1)
                    turn_x(0, 0)
                    turn_x(1, 1)
                    hidden(0, 0, expert(pe, 0))
                    pair_loop(pe, step)

                @block.scalar
                def _(act):
                    def copy_x(j, k):
                        act.wait_ge(xt_turned, j + 1)
                        past(act, h_ready, j - 1)
                        act.copy(flat(xt[k][:]), ps[k][:, 0:D]).then_inc(xt_ready, 1)

                    def gelu(j, k):
                        act.wait_ge(h_biased, j + 1)
                        past(act, h_turned, j - 1)
                        act.activation(hg[k][:], hb[k][:], ACT.Gelu).then_inc(h_done, 1)

                    def step(j, k):
                        act.wait_ge(h_turned, j + 1)
                        past(act, y_ready, j - 1)
                        act.copy(flat(ht[k][:]), ps[4 + k][:, 0:HID]).then_inc(ht_ready, 1)
                        gelu(j + 1, 1 - k)
                        copy_x(j + 2, k)
                    copy_x(0, 0)
                    copy_x(1, 1)
                    gelu(0, 0)
                    pair_loop(act, step)

                @block.vector
                def _(dve):
                    def bias(j, k, e):
                        dve.wait_ge(h_ready, j + 1)
                        past(dve, h_done, j - 1)
                        dve.tensor_tensor(hb[k][:], ps[2 + k][:], flat(b1[:, bass.ds(e, 1), :]), ALU.add
                                          ).then_inc(h_biased, 1)

                    def step(j, k):
                        e_next, e = expert(dve, j + 1), expert(dve, j)
                        bias(j + 1, 1 - k, e_next)
                        dve.wait_ge(y_ready, j + 1)
                        past(dve, y_stored[k], (j - k) * 8)
                        dve.tensor_tensor(yo[k][:], ps[6 + k][:, 0:D], flat(b2[:, bass.ds(e, 1), :]), ALU.add
                                          ).then_inc(y_biased, 1)
                    bias(0, 0, expert(dve, 0))
                    pair_loop(dve, step)

        with ExitStack() as c12:
            RY = 4
            got = [[c12.enter_context(nc.sbuf_tensor(f"got{i}_{k}", [P, D], F32)) for k in range(RY)] for i in range(2)]
            fetched = [[gsem(f"fetched{i}_{k}") for k in range(RY)] for i in range(2)]
            summed, half, out_stored = sem("summed"), sem("half"), gsem("out_stored")
            with nc.Block() as block:
                @block.gpsimd
                def _(pool):
                    def send(n):
                        r = P if n < NT - 1 else LAST
                        pool.wait_ge(summed, n + 1)
                        pool.indirect_dma_start(
                            out, bass.IndirectOffsetOnAxis(ap=nodeid[0:r, n:n + 1].bitcast(U32), axis=0),
                            xin[0:r, n, 0:D], None).then_inc(out_stored, 16)
                    for n in range(NT):
                        k, r = n % RY, P if n < NT - 1 else LAST
                        if n >= RY:
                            pool.wait_ge(summed, n - RY + 1)
                        for i in range(2):
                            pool.indirect_dma_start(
                                got[i][k][0:r, :], None, y_dram,
                                bass.IndirectOffsetOnAxis(ap=place[i][0:r, n:n + 1].bitcast(U32), axis=0)
                            ).then_inc(fetched[i][k], 16)
                        if n >= RY - 1:
                            send(n - RY + 1)
                    for n in range(NT - RY + 1, NT):
                        send(n)
                    pool.wait_ge(out_stored, 16 * NT)

                @block.vector
                def _(dve):
                    for n in range(NT):
                        k, r = n % RY, P if n < NT - 1 else LAST
                        row = xin[0:r, n, 0:D]
                        dve.wait_ge(fetched[0][k], 16 * (n // RY + 1))
                        dve.scalar_tensor_tensor(row, got[0][k][0:r, :], weight[0:r, 0, n:n + 1], row, ALU.mult, ALU.add
                                                 ).then_inc(half, 1)
                        dve.wait_ge(fetched[1][k], 16 * (n // RY + 1))
                        dve.wait_ge(half, n + 1)
                        dve.scalar_tensor_tensor(row, got[1][k][0:r, :], weight[0:r, 1, n:n + 1], row, ALU.mult, ALU.add
                                                 ).then_inc(summed, 1)


NAMES = ["x", "src", "dst", "L0_gnn_thetas", "L0_gnn_phis", "L0_gnn_gammas", "L0_gnn_betas",
         "L0_mix_wq", "L0_mix_bq", "L0_mix_wk", "L0_mix_bk", "L0_mix_wv", "L0_mix_bv", "L0_mix_wo", "L0_mix_bo",
         "L0_ffn_gamma", "L0_ffn_beta", "L0_ffn_Wr", "L0_ffn_br", "L0_ffn_W1", "L0_ffn_b1", "L0_ffn_W2", "L0_ffn_b2"]


def kernel(**inputs):
    from concourse import bacc
    from concourse.bass_utils import run_bass_kernel_spmd

    nc = bacc.Bacc("TRN2", target_bir_lowering=False, num_devices=1)
    arrays, t = {}, {}
    for name in NAMES:
        a = np.ascontiguousarray(inputs[name])
        arrays[f"in_{name}"] = a
        t[name] = nc.dram_tensor(f"in_{name}", a.shape, mybir.dt.from_np(a.dtype), kind="ExternalInput").ap()
    out = nc.dram_tensor("out", (N, D), F32, kind="ExternalOutput").ap()
    build(nc, t, out)
    return run_bass_kernel_spmd(nc, [arrays], core_ids=[0]).results[0]["out"]
```

```python
from contextlib import ExitStack

import numpy as np

import concourse.bass as bass
from concourse import mybir

F32 = mybir.dt.float32
F16 = mybir.dt.float16
I32 = mybir.dt.int32
U32 = mybir.dt.uint32
ALU = mybir.AluOpType
ACT = mybir.ActivationFunctionType
AX_X = mybir.AxisListType.X
RMAX = bass.bass_isa.ReduceOp.max

P = 128
N = 3125
D = 256
H2 = D // P
NT = -(-N // P)
NP = NT * P
LAST = N - (NT - 1) * P
NE = 50000
EB = 125
NB = NE // EB
CB = 20
NC = NB // CB
LAYERS = 3
MID = NP // 2
ROWS = NP + 1
K = 8
WIN = 56 * K
NW = -(-(NE + NE // P + 2 * NT) // WIN)
NEG = -3.0e38
DEGCAP = 4095
HEADS = 8
DH = D // HEADS
EXPERTS = 8
HID = 512
EPS = 1e-5
U = 5


def build(nc, t, out):
    ctx = ExitStack()
    with ctx:
        def sb(name, shape, dt=F32):
            return ctx.enter_context(nc.sbuf_tensor(name, shape, dt))

        phase_sems = []

        def sem(name):
            phase_sems.append(nc.alloc_semaphore(name=name))
            return phase_sems[-1]

        gather_sems = {}

        def gsem(name):
            if name not in gather_sems:
                gather_sems[name] = nc.alloc_semaphore(name=name)
            return gather_sems[name]

        def end_phase():
            with nc.Block() as block:
                @block.gpsimd
                def _(pool):
                    for s in phase_sems:
                        pool.sem_clear(s)
            for s in phase_sems:
                nc.release_semaphore(s)
            phase_sems.clear()

        ps = [ctx.enter_context(nc.psum_tensor(f"bank{i}", [P, 512], F32)) for i in range(8)]

        def dram(name, shape, dt=F32):
            return nc.dram_tensor(name, shape, dt).ap()

        x_perm = dram("x_perm", (NP, D + 1))
        lo_dram = dram("lo_dram", (NE,), F16)
        key_dram = dram("key_dram", (P, NT))
        table_dram = dram("table_dram", (NW, P, WIN), I32)
        tile_dram = dram("tile_dram", (NW, WIN), I32)
        a_rows = [dram(f"a_rows{l}", (ROWS, D)) for l in range(LAYERS)]

        held = ctx.enter_context(nc.semaphore("held"))

        def hold(eng, semaphore, value):
            eng.wait_ge(semaphore, value)
            eng.sem_inc(held, 1)

        iota = sb("iota", [P, WIN], F16)
        iota_p = sb("iota_p", [P, 1])
        ident = sb("ident", [P, P])
        rowid = sb("rowid", [P, NT], I32)
        nodeid = sb("nodeid", [P, NT], I32)
        xin = sb("xin", [P, NT, D + 1])
        nwin = sb("nwin", [1, 1], I32)
        nstep = sb("nstep", [1, P], I32)
        slotbase = sb("slotbase", [P, NT + 1])

        c2 = ExitStack()
        ctx.callback(c2.close)

        def sb2(name, shape, dt=F32):
            return c2.enter_context(nc.sbuf_tensor(name, shape, dt))

        oh_hi = sb2("oh_hi", [EB, NB, NT], F16)
        dv_e = sb2("dv_e", [EB, NB])
        hist = sb2("hist", [P, NB, NT], F16)
        nbase = sb2("nbase", [P, NT])
        q_h = sb2("q_h", [P, NT], F16)

        with ExitStack() as c1:
            def sb1(name, shape, dt=F32):
                return c1.enter_context(nc.sbuf_tensor(name, shape, dt))
            q4 = NB // 100
            src_r = sb1("src_r", [100, q4, EB], I32)
            dst_r = sb1("dst_r", [100, q4, EB], I32)
            lo_i = sb1("lo_i", [100, q4, EB], I32)
            hi_i = sb1("hi_i", [100, q4, EB], I32)
            lo_f = sb1("lo_f", [100, q4, EB])
            hi_f = sb1("hi_f", [100, q4, EB])
            dv_f = sb1("dv_f", [100, q4, EB])
            dv_g = sb1("dv_g", [100, q4, EB])
            lo_h = sb1("lo_h", [100, q4, EB], F16)
            lo_e = sb1("lo_e", [EB, NB], F16)
            hi_e = sb1("hi_e", [EB, NB], F16)
            oh_lo = [sb1(f"oh_lo{i}", [EB, CB, P], F16) for i in range(2)]
            zero = sb1("zero", [P, P + NT], F16)
            deg = sb1("deg", [P, NT])
            iota_i = sb1("iota_i", [P, NT], I32)
            node_f = sb1("node_f", [P, NT])
            key = sb1("key", [P, NT])
            key_all = sb1("key_all", [P, NP])
            rank = sb1("rank", [P, NT])
            junk = sb1("junk", [P, NP])
            rank_i = sb1("rank_i", [P, NT], I32)
            RV = 14
            neg_key = sb1("neg_key", [P, NT])
            signs = sb1("signs", [P, NT - RV])
            sign_junk = sb1("sign_junk", [P, NP])
            neg_made1, signs_summed = sem("neg_made1"), sem("signs_summed")
            tq_i = sb1("tq_i", [P, 2, NT], I32)
            tq_f = sb1("tq_f", [P, 2, NT])
            idv = sb1("idv", [P, NT], I32)
            ge = sb1("ge", [P, NT])
            idf = sb1("idf", [P, NT])
            sel3 = sb1("sel3", [P, NT, NT])
            tmax = sb1("tmax", [P, NT])
            tmax_all = sb1("tmax_all", [P, NT])
            zeros25 = sb1("zeros25", [P, NT])
            steps_f = sb1("steps_f", [1, P])
            small = sb1("small", [1, 4])
            small_i = sb1("small_i", [1, 2], I32)
            wf = sb1("wf", [1, P])

            loaded, loaded_x = sem("loaded"), sem("loaded_x")
            made = sem("made")
            dve1 = sem("dve1")
            turned, oh_ready, oh_used = sem("turned"), sem("oh_ready"), sem("oh_used")
            hist_ready, hist_used = sem("hist_ready"), sem("hist_used")
            lo_stored, key_stored, key_loaded = sem("lo_stored"), sem("key_stored"), sem("key_loaded")
            degree_ready = sem("degree_ready")
            tmax_ready, tmax_done = sem("tmax_ready"), sem("tmax_done")
            scattered = gsem("scattered")

            n_consts = 8
            pad_cleared, lo_made, key_made, places_made = (sem("pad_cleared"), sem("lo_made"), sem("key_made"),
                                                           sem("places_made"))
            columns_made = sem("columns_made")
            with nc.Block() as block:
                @block.gpsimd
                def _(pool):
                    pool.iota(iota[:], [[1, WIN]], base=0, channel_multiplier=0,
                              allow_small_or_imprecise_dtypes=True).then_inc(made, 1)
                    pool.iota(iota_p[:], [[0, 1]], base=0, channel_multiplier=1,
                              allow_small_or_imprecise_dtypes=True).then_inc(made, 1)
                    pool.iota(iota_i[:], [[P, NT]], base=0, channel_multiplier=1).then_inc(made, 1)
                    pool.iota(wf[:], [[WIN // K, P]], base=0, channel_multiplier=0,
                              allow_small_or_imprecise_dtypes=True).then_inc(made, 1)
                    pool.memset(ident[:], 0.0).then_inc(made, 1)
                    pool.wait_ge(made, 5)
                    pool.affine_select(out=ident[:], in_=ident[:], compare_op=ALU.not_equal, fill=1.0, base=0,
                                       pattern=[[-1, P]], channel_multiplier=1).then_inc(made, 1)
                    pool.memset(zero[:], 0.0).then_inc(made, 1)
                    pool.memset(zeros25[:], 0.0).then_inc(made, 1)
                    pool.wait_ge(tmax_ready, 1)
                    pool.partition_all_reduce(tmax_all[:], tmax[:], P, RMAX).then_inc(tmax_done, 1)
                    pool.wait_ge(loaded_x, 32)
                    pool.wait_ge(places_made, 1)
                    for h in range(NT):
                        pool.indirect_dma_start(
                            x_perm, bass.IndirectOffsetOnAxis(ap=rank_i[:, h:h + 1].bitcast(U32), axis=0),
                            xin[:, h, :], None).then_inc(scattered, 16)
                    pool.wait_ge(scattered, 16 * NT)

                @block.sync
                def _(sp):
                    r = "(g r e) -> r g e"
                    sp.dma_start(src_r[:], t["src"].rearrange(r, g=q4, r=100)).then_inc(loaded, 16)
                    sp.dma_start(dst_r[:], t["dst"].rearrange(r, g=q4, r=100)).then_inc(loaded, 16)
                    sp.dma_start(xin[:, 0:NT - 1, 0:D],
                                 t["x"][0:(NT - 1) * P, :].rearrange("(h p) d -> p h d", p=P)).then_inc(loaded_x, 16)
                    sp.wait_ge(pad_cleared, 1)
                    sp.dma_start(xin[0:LAST, NT - 1, 0:D], t["x"][(NT - 1) * P:N, :]).then_inc(loaded_x, 16)
                    sp.wait_ge(lo_made, 1)
                    sp.dma_start(lo_dram.rearrange(r, g=q4, r=100), lo_h[:]).then_inc(lo_stored, 16)
                    sp.wait_ge(key_made, 1)
                    sp.dma_start(key_dram, key[:]).then_inc(key_stored, 16)
                    sp.wait_ge(key_stored, 16)
                    sp.dma_start(key_all[:], key_dram.rearrange("p t -> (p t)").partition_broadcast(P)
                                 ).then_inc(key_loaded, 16)
                    sp.wait_ge(lo_stored, 16)

                @block.tensor
                def _(pe):
                    pe.wait_ge(made, 6)
                    for i, (a, bank) in enumerate(((lo_f, 0), (hi_f, 1), (dv_f, 2))):
                        pe.wait_ge(columns_made, i + 1)
                        for g in range(q4):
                            mm = pe.transpose(ps[bank][0:EB, g * 100:(g + 1) * 100], a[:, g, :], ident[0:100, 0:100])
                        mm.then_inc(turned, 1)
                    pe.wait_ge(made, n_consts)
                    pe.matmul(ps[3][:, 0:NT], zero[:, 0:P], zero[:, P:P + NT], start=True, stop=False,
                              skip_group_check=True)
                    with pe.Fori(0, NC // 2) as j:
                        for i in range(2):
                            pe.wait_ge(oh_ready, 2 * j + i + 1)
                            pe.wait_ge(hist_used, 2 * j + i + 1)
                            for b in range(CB):
                                c = (2 * j + i) * CB + b
                                rhs = oh_hi[:, bass.ds(c, 1), :].rearrange("e a b -> e (a b)")
                                pe.matmul(ps[3][:, 0:NT], oh_lo[i][:, b, :], rhs,
                                          start=False, stop=False, skip_group_check=True)
                                mm = pe.matmul(ps[4 + i][:, b * NT:(b + 1) * NT], oh_lo[i][:, b, :], rhs,
                                               start=True, stop=True, skip_group_check=True)
                            mm.then_inc(hist_ready, 1)
                    pe.matmul(ps[3][:, 0:NT], zero[:, 0:P], zero[:, P:P + NT], start=False, stop=True,
                              skip_group_check=True).then_inc(degree_ready, 1)

                @block.scalar
                def _(act):
                    act.sem_inc(hist_used, 2)
                    with act.Fori(0, NC // 2) as j:
                        for i in range(2):
                            act.wait_ge(hist_ready, 2 * j + i + 1)
                            act.copy(hist[:, bass.ds((2 * j + i) * CB, CB), :].rearrange("p a b -> p (a b)"),
                                     ps[4 + i][:, 0:CB * NT]).then_inc(hist_used, 1)
                    act.wait_ge(neg_made1, 1)
                    act.wait_ge(key_loaded, 16)
                    for h in range(RV, NT):
                        if h > RV:
                            act.wait_ge(signs_summed, h - RV)
                        act.activation(sign_junk[:], key_all[:], ACT.Sign, bias=neg_key[:, h:h + 1],
                                       accum_out=signs[:, h - RV:h - RV + 1]).then_inc(signs_summed, 1)

                @block.vector
                def _(dve):
                    count = [0]

                    def step(ins, made=None):
                        ins.then_inc(dve1, 1)
                        count[0] += 1
                        dve.wait_ge(dve1, count[0])
                        if made is not None:
                            dve.sem_inc(made, 1)

                    dve.memset(junk[:], 0.0)
                    step(dve.memset(xin[:, NT - 1, :], 0.0), pad_cleared)
                    dve.wait_ge(loaded, 32)
                    dve.tensor_scalar(lo_i[:], src_r[:], P - 1, None, ALU.bitwise_and)
                    step(dve.tensor_scalar(hi_i[:], src_r[:], 7, None, ALU.logical_shift_right))
                    step(dve.tensor_copy(lo_h[:], lo_i[:]), lo_made)
                    step(dve.tensor_copy(lo_f[:], lo_i[:]), columns_made)
                    step(dve.tensor_copy(hi_f[:], hi_i[:]), columns_made)
                    step(dve.tensor_scalar(dv_g[:], dst_r[:], float(MID), None, ALU.is_ge))
                    step(dve.scalar_tensor_tensor(dv_f[:], dst_r[:], float(MID), dv_g[:], ALU.subtract, ALU.add), columns_made)
                    dve.wait_ge(turned, 3)
                    dve.tensor_copy(lo_e[:], ps[0][0:EB, 0:NB])
                    dve.tensor_copy(dv_e[:], ps[2][0:EB, 0:NB])
                    step(dve.tensor_copy(hi_e[:], ps[1][0:EB, 0:NB]))
                    dve.wait_ge(made, n_consts)
                    step(dve.tensor_tensor(oh_hi[:], iota[0:EB, 0:NT].unsqueeze(1).broadcast_to([EB, NB, NT]),
                                           hi_e[:].unsqueeze(2).broadcast_to([EB, NB, NT]), ALU.is_equal))
                    with dve.Fori(0, NC // 2) as j:
                        for i in range(2):
                            dve.wait_ge(hist_used, 2 * j + i + 1)
                            dve.tensor_tensor(
                                oh_lo[i][:], iota[0:EB, 0:P].unsqueeze(1).broadcast_to([EB, CB, P]),
                                lo_e[:, bass.ds((2 * j + i) * CB, CB)].unsqueeze(2).broadcast_to([EB, CB, P]),
                                ALU.is_equal).then_inc(oh_ready, 1)
                    dve.wait_ge(degree_ready, 1)
                    dve.tensor_copy(node_f[:], iota_i[:])
                    step(dve.tensor_copy(deg[:], ps[3][:, 0:NT]))
                    step(dve.tensor_scalar(key[:], deg[:], float(DEGCAP), float(DEGCAP + 1), ALU.min, ALU.mult))
                    step(dve.tensor_tensor(key[:], key[:], node_f[:], ALU.subtract), key_made)
                    step(dve.tensor_scalar(neg_key[:], key[:], -1.0, None, ALU.mult), neg_made1)
                    step(dve.tensor_scalar(ge[:], node_f[:], float(MID), None, ALU.is_ge))
                    step(dve.tensor_tensor(idf[:], node_f[:], ge[:], ALU.add))
                    step(dve.tensor_copy(idv[:], idf[:]))
                    step(dve.tensor_copy(xin[:, :, D:D + 1].bitcast(I32), idv[:].unsqueeze(2)))
                    dve.wait_ge(key_loaded, 16)
                    for h in range(RV):
                        ins = dve.tensor_scalar(junk[:], key_all[:], key[:, h:h + 1], None, ALU.is_gt, ALU.add,
                                                accum_out=rank[:, h:h + 1])
                        step(ins)
                    dve.wait_ge(signs_summed, NT - RV)
                    step(dve.tensor_scalar(rank[:, RV:NT], signs[:], float(NP - 1), 0.5, ALU.add, ALU.mult))
                    step(dve.tensor_copy(rank_i[:], rank[:]), places_made)
                    step(dve.tensor_scalar(tq_i[:, 0, :], rank_i[:], 7, None, ALU.logical_shift_right))
                    step(dve.tensor_scalar(tq_i[:, 1, :], rank_i[:], P - 1, None, ALU.bitwise_and))
                    step(dve.tensor_copy(tq_f[:], tq_i[:]))
                    step(dve.tensor_copy(q_h[:], tq_f[:, 1, :]))
                    shape = [P, NT, NT]
                    step(dve.tensor_tensor(sel3[:], iota[:, 0:NT].unsqueeze(2).broadcast_to(shape),
                                           tq_f[:, 0, :].unsqueeze(1).broadcast_to(shape), ALU.is_equal))
                    step(dve.tensor_tensor(sel3[:], sel3[:], deg[:].unsqueeze(1).broadcast_to(shape), ALU.mult))
                    step(dve.tensor_reduce(tmax[:], sel3[:], AX_X, ALU.max))
                    dve.sem_inc(tmax_ready, 1)
                    dve.wait_ge(tmax_done, 1)
                    step(dve.memset(slotbase[:, 0:1], 0.0))
                    step(dve.tensor_tensor_scan(slotbase[:, 1:NT + 1], tmax_all[:], zeros25[:], 0.0, ALU.add, ALU.add))
                    step(dve.tensor_tensor(sel3[:], iota[:, 0:NT].unsqueeze(1).broadcast_to(shape),
                                           tq_f[:, 0, :].unsqueeze(2).broadcast_to(shape), ALU.is_equal))
                    step(dve.tensor_tensor(sel3[:], sel3[:], slotbase[:, 0:NT].unsqueeze(1).broadcast_to(shape), ALU.mult))
                    step(dve.tensor_reduce(nbase[:], sel3[:], AX_X, ALU.add))
                    spw = WIN // K
                    step(dve.tensor_scalar(small[:, 0:1], slotbase[0:1, NT:NT + 1], float(K - 1), None, ALU.add))
                    step(dve.tensor_copy(small_i[:, 0:1], small[:, 0:1]))
                    step(dve.tensor_scalar(small_i[:, 1:2], small_i[:, 0:1], K.bit_length() - 1, None,
                                           ALU.logical_shift_right))
                    step(dve.tensor_copy(small[:, 0:1], small_i[:, 1:2]))
                    step(dve.tensor_scalar(steps_f[:], wf[:], small[:, 0:1], None, ALU.is_lt))
                    step(dve.tensor_reduce(small[:, 1:2], steps_f[:], AX_X, ALU.add))
                    step(dve.tensor_copy(nwin[:], small[:, 1:2]))
                    step(dve.tensor_scalar(wf[:], wf[:], small[:, 0:1], -1.0, ALU.subtract, ALU.mult))
                    step(dve.tensor_scalar(wf[:], wf[:], 1.0, float(spw), ALU.max, ALU.min))
                    step(dve.tensor_copy(nstep[:], wf[:]))

        end_phase()

        with ExitStack() as c3:
            def sb3(name, shape, dt=F32):
                return c3.enter_context(nc.sbuf_tensor(name, shape, dt))
            xpre = sb3("xpre", [P, NB, NT])
            lo_bc = [sb3(f"lo_bc{i}", [P, CB * EB], F16) for i in range(2)]
            lot = [sb3(f"lot{i}", [P, CB, EB], F16) for i in range(2)]
            xc = [sb3(f"xc{i}", [P, CB * NT]) for i in range(2)]
            xw = [sb3(f"xw{i}", [P, CB, 2, NT], F16) for i in range(2)]
            earlier = sb3("earlier", [EB, EB], F16)
            eqm = [sb3(f"eqm{i}", [EB, 4, EB], F16) for i in range(2)]
            rm = [sb3(f"rm{i}", [EB, CB // 2, 2, NT]) for i in range(2)]
            gq = [sb3(f"gq{i}", [EB, CB, 2]) for i in range(2)]
            RG = 10
            hot0 = 2 * CB
            far = [sb3(f"far{i}", [EB, 12, P], F16) for i in range(2)]
            ohq = [sb3(f"ohq{i}", [EB, CB, P], F16) for i in range(2)]
            ohg = [sb3(f"ohg{i}", [EB, WIN], F16) for i in range(RG)]
            wshift = sb3("wshift", [P, 1])
            zscan = sb3("zscan", [P, 1])
            zero2 = sb3("zero2", [EB, WIN], F16)
            tab_f = sb3("tab_f", [P, WIN])
            tab_i = sb3("tab_i", [P, WIN], I32)
            gnum_i = sb3("gnum_i", [WIN // 4, 4], I32)
            gnum = sb3("gnum", [WIN // 4, 4])
            tcmp = sb3("tcmp", [WIN // 4, 4, NT - 1])
            tsum = sb3("tsum", [WIN // 4, 4])
            tof = sb3("tof", [WIN // 4, 4], I32)

            made2, dve2 = sem("made2"), sem("dve2")
            lo_loaded = [sem(f"lo_loaded{i}") for i in range(2)]
            lot_ready, eq_ready, eq_masked, xc_ready = sem("lot_ready"), sem("eq_ready"), sem("eq_masked"), sem("xc_ready")
            r_ready, r_read, gq_ready = sem("r_ready"), sem("r_read"), sem("gq_ready")
            far_ready, ohq_ready, ohg_ready, hot_used = sem("far_ready"), sem("ohq_ready"), sem("ohg_ready"), sem("hot_used")
            win_done, win_read = sem("win_done"), sem("win_read")
            table_chain = sem("table_chain")
            table_made, table_stored = sem("table_made"), sem("table_stored")
            QD = CB // 4

            def chunk_steps(eng, step):
                with eng.Fori(0, NC // 2 - 2) as j:
                    for i in range(2):
                        step(2 * j + i, i, True, True)
                for c in range(NC - 4, NC):
                    step(c, c % 2, c + 2 < NC, c + 3 < NC)

            with nc.Block() as block:
                @block.gpsimd
                def _(pool):
                    pool.iota(gnum_i[:], [[1, 4]], base=0, channel_multiplier=4).then_inc(made2, 1)
                    pool.memset(earlier[:], 1.0).then_inc(made2, 1)
                    pool.wait_ge(made2, 2)
                    pool.affine_select(out=earlier[:], in_=earlier[:], compare_op=ALU.is_gt, fill=0.0, base=0,
                                       pattern=[[1, EB]], channel_multiplier=-1).then_inc(made2, 1)

                @block.sync
                def _(sp):
                    windows = sp.value_load(nwin[0:1, 0:1], min_val=1, max_val=NW)
                    with sp.Fori(0, windows) as w:
                        with sp.Fori(0, NC // 2) as j:
                            for i in range(2):
                                hold(sp, lot_ready, w * NC + 2 * j + i + 1)
                                sp.dma_start(lo_bc[i][:], lo_dram[bass.ds((2 * j + i) * (CB * EB), CB * EB)]
                                             .partition_broadcast(P)).then_inc(lo_loaded[i], 16)
                        hold(sp, table_made, w + 1)
                        sp.dma_start(table_dram[bass.ds(w, 1)].rearrange("o p g -> (o p) g"), tab_i[:]
                                     ).then_inc(table_stored, 16)
                        sp.dma_start(tile_dram[bass.ds(w, 1)].rearrange("o (p g) -> (o p) g", g=4), tof[:]
                                     ).then_inc(table_stored, 16)
                        hold(sp, table_stored, w * 32 + 32)

                @block.tensor
                def _(pe):
                    def look_up(cc, i):
                        pe.wait_ge(lot_ready, cc + 3)
                        pe.wait_ge(r_read, cc + 1)
                        for b in range(CB):
                            r = ps[2 + 2 * i + b // 10][0:EB, (b % 10) * 2 * NT:(b % 10 + 1) * 2 * NT]
                            pe.matmul(r, lot[i][:, b, :], xw[i][:, b, :, :].rearrange("p a b -> p (a b)"),
                                      start=b % 10 == 0, stop=False, skip_group_check=True)

                    def pairs(cc, i, qd):
                        for b in range(4):
                            one = lot[i][:, 4 * qd + b, :]
                            mm = pe.matmul(ps[qd % 2][0:EB, b * EB:(b + 1) * EB], one, one,
                                           start=True, stop=True, skip_group_check=True)
                        mm.then_inc(eq_ready, 1)

                    def before(cc, c, i, qd):
                        pe.wait_ge(eq_masked, cc * QD + qd + 1)
                        for b in range(4 * qd, 4 * qd + 4):
                            r = ps[2 + 2 * i + b // 10][0:EB, (b % 10) * 2 * NT:(b % 10) * 2 * NT + NT]
                            rhs = oh_hi[:, bass.ds(c * CB + b, 1), :].rearrange("e a b -> e (a b)")
                            mm = pe.matmul(r, eqm[qd % 2][:, b % 4, :], rhs, start=False,
                                           stop=b % 10 == 9, skip_group_check=True)
                        if qd == QD - 1:
                            mm.then_inc(r_ready, 1)

                    windows = pe.value_load(nwin[0:1, 0:1], min_val=1, max_val=NW)
                    with pe.Fori(0, windows) as w:
                        def front(cc, c, i, tables):
                            look_up(cc, i)
                            pairs(cc, i, 0)
                            pairs(cc, i, 1)
                            for qd in range(QD):
                                tables(qd)
                                before(cc, c, i, qd)
                                if qd + 2 < QD:
                                    pairs(cc, i, qd + 2)

                        def step(c, i, fronts, loads):
                            cc = w * NC + c

                            def tables(qd):
                                if qd % 3 == 0:
                                    pe.wait_ge(ohq_ready, cc * 2 + qd // 3 + 1)
                                for b in range(4 * qd, 4 * qd + 4):
                                    pe.wait_ge(ohg_ready, cc * CB + b + 1)
                                    pe.matmul(ps[7][:, 0:WIN], ohq[i][:, b, :], ohg[b % RG][:], start=False, stop=False,
                                              skip_group_check=True).then_inc(hot_used, 1)
                            if fronts:
                                front(cc + 2, c + 2, i, tables)
                            else:
                                for qd in range(QD):
                                    tables(qd)

                        pe.wait_ge(win_read, w + 1)
                        pe.matmul(ps[7][:, 0:WIN], zero2[:, 0:P], zero2[:, 0:WIN], start=True, stop=False,
                                  skip_group_check=True)
                        front(w * NC, 0, 0, lambda qd: None)
                        front(w * NC + 1, 1, 1, lambda qd: None)
                        chunk_steps(pe, step)
                        pe.matmul(ps[7][:, 0:WIN], zero2[:, 0:P], zero2[:, 0:WIN], start=False, stop=True,
                                  skip_group_check=True).then_inc(win_done, 1)

                @block.scalar
                def _(act):
                    windows = act.value_load(nwin[0:1, 0:1], min_val=1, max_val=NW)
                    with act.Fori(0, windows) as w:
                        def step(c, i, fronts, loads):
                            cc = w * NC + c
                            act.wait_ge(gq_ready, cc + 1)
                            for hb in range(2):
                                b0, b1 = (0, 12) if hb == 0 else (12, CB)
                                for b in range(b0, b1):
                                    ins = act.activation(far[hb][:, b - b0, :], iota[0:EB, 0:P], ACT.Abs,
                                                         bias=gq[i][:, b, 1:2], scale=-1.0)
                                ins.then_inc(far_ready, 1)
                                act.wait_ge(far_ready, cc * 2 + hb + 1)
                                act.wait_ge(hot_used, cc * CB + hot0 - 2 * CB + b1)
                                act.activation(ohq[i][:, b0:b1, :], far[hb][:, 0:b1 - b0, :], ACT.Relu, bias=1.0,
                                               scale=-1.0).then_inc(ohq_ready, 1)
                        chunk_steps(act, step)

                @block.vector
                def _(dve):
                    count = [0]

                    def step1(ins):
                        ins.then_inc(dve2, 1)
                        count[0] += 1
                        dve.wait_ge(dve2, count[0])

                    windows = dve.value_load(nwin[0:1, 0:1], min_val=1, max_val=NW)
                    dve.sem_inc(lot_ready, 2)
                    dve.sem_inc(r_read, 2)
                    dve.sem_inc(hot_used, hot0)
                    step1(dve.memset(zscan[:], 0.0))
                    dve.memset(zero2[:], 0.0)
                    for i in range(2):
                        dve.tensor_copy(xw[i][:, :, 1, :], q_h[:].unsqueeze(1).broadcast_to([P, CB, NT]))
                    dve.memset(wshift[:], 0.0)
                    dve.tensor_copy(xpre[:, 0, :], nbase[:])
                    for h in range(NT):
                        dve.tensor_tensor_scan(xpre[:, 1:NB, h], hist[:, 0:NB - 1, h],
                                               zscan[:].broadcast_to([P, NB - 1]), nbase[:, h:h + 1],
                                               ALU.add, ALU.add)
                    dve.wait_ge(made2, 3)
                    step1(dve.tensor_copy(gnum[:], gnum_i[:]))
                    dve.sem_inc(win_read, 1)
                    with dve.Fori(0, windows) as w:
                        def one_hots(c, i):
                            cc = w * NC + c
                            dve.tensor_scalar(xc[i][:], xpre[:, bass.ds(c * CB, CB), :]
                                              .rearrange("p a b -> p (a b)"), wshift[:, 0:1], -256.0,
                                              ALU.subtract, ALU.max).then_inc(xc_ready, 1)
                            dve.wait_ge(lo_loaded[i], (w * NC + c - i) * 8 + 16)
                            dve.tensor_scalar(lot[i][:].rearrange("p a b -> p (a b)"), lo_bc[i][:],
                                              iota_p[:, 0:1], None, ALU.is_equal)
                            dve.wait_ge(xc_ready, cc + 1)
                            dve.tensor_scalar(xw[i][:, :, 0, :], xc[i][:].rearrange("p (a b) -> p a b", b=NT), 768.0, None,
                                              ALU.min).then_inc(lot_ready, 1)

                        def mask(cc, qd):
                            dve.wait_ge(eq_ready, cc * QD + qd + 1)
                            dve.tensor_tensor(eqm[qd % 2][:], ps[qd % 2][0:EB, 0:4 * EB]
                                              .rearrange("p (a b) -> p a b", a=4),
                                              earlier[:].unsqueeze(1).broadcast_to([EB, 4, EB]),
                                              ALU.mult).then_inc(eq_masked, 1)

                        def pick(cc, c, i):
                            dve.wait_ge(r_ready, cc + 1)
                            for hb in range(2):
                                c0 = bass.ds(c * CB + hb * (CB // 2), CB // 2)
                                ins = dve.tensor_tensor(
                                    rm[hb][:], ps[2 + 2 * i + hb][0:EB, 0:CB * NT]
                                    .rearrange("p (a c b) -> p a c b", c=2, b=NT),
                                    oh_hi[:, c0, :].unsqueeze(2).broadcast_to([EB, CB // 2, 2, NT]), ALU.mult)
                            ins.then_inc(r_read, 1)
                            dve.wait_ge(r_read, cc + 3)
                            for hb in range(2):
                                ins = dve.tensor_reduce(gq[i][:, hb * (CB // 2):(hb + 1) * (CB // 2), :], rm[hb][:],
                                                        AX_X, ALU.add)
                            ins.then_inc(gq_ready, 1)

                        def step(c, i, fronts, loads):
                            cc = w * NC + c
                            dve.wait_ge(gq_ready, cc + 1)
                            for qd in range(QD):
                                if fronts:
                                    mask(cc + 2, qd)
                                for b in range(4 * qd, 4 * qd + 4):
                                    dve.wait_ge(hot_used, cc * CB + b + 1 - RG + hot0)
                                    dve.tensor_scalar(ohg[b % RG][:], iota[0:EB, :], gq[i][:, b, 0:1],
                                                      dv_e[:, bass.ds(c * CB + b, 1)], ALU.is_equal, ALU.mult
                                                      ).then_inc(ohg_ready, 1)
                            if loads:
                                one_hots(c + 3, 1 - i)
                            if fronts:
                                dve.wait_ge(ohq_ready, cc * 2 + 2)
                                pick(cc + 2, c + 2, i)

                        for c in range(3):
                            one_hots(c, c % 2)
                            if c < 2:
                                for qd in range(QD):
                                    mask(w * NC + c, qd)
                                pick(w * NC + c, c, c)
                        chunk_steps(dve, step)
                        dve.wait_ge(win_done, w + 1)
                        dve.tensor_scalar(tab_i[:], ps[7][:, 0:WIN], float(MID), None, ALU.add).then_inc(win_read, 1)
                        dve.tensor_tensor(tcmp[:], slotbase[0:WIN // 4, 1:NT].unsqueeze(1).broadcast_to([WIN // 4, 4, NT - 1]),
                                          gnum[:].unsqueeze(2).broadcast_to([WIN // 4, 4, NT - 1]),
                                          ALU.is_le).then_inc(table_chain, 1)
                        dve.wait_ge(table_chain, w * 2 + 1)
                        dve.tensor_reduce(tsum[:], tcmp[:], AX_X, ALU.add).then_inc(table_chain, 1)
                        dve.wait_ge(table_chain, w * 2 + 2)
                        dve.tensor_scalar(wshift[:], wshift[:], float(WIN), None, ALU.add)
                        dve.tensor_scalar(gnum[:], gnum[:], float(WIN), None, ALU.add)
                        dve.tensor_scalar(tof[:], tsum[:], float(D), None, ALU.mult).then_inc(table_made, 1)
                        dve.wait_ge(table_made, w + 1)
        c2.close()
        end_phase()

        c4 = ExitStack()
        ctx.callback(c4.close)

        def sb4(name, shape, dt=F32):
            return c4.enter_context(nc.sbuf_tensor(name, shape, dt))

        w_ab = sb4("w_ab", [P, LAYERS, H2, 2 * D])
        b_rows = sb4("b_rows", [P, NT, D])
        f_t = sb4("f_t", [P, H2, NP])
        xs = [sb4(f"xs{k}", [P, H2, P]) for k in range(U)]
        a_st = [sb4(f"a_st{k}", [P, D]) for k in range(U)]
        a_idx = [sb4(f"a_idx{k}", [P, 1], I32) for k in range(U)]
        bn_w = sb4("bn_w", [P, 2, LAYERS, H2])
        ring = [sb4(f"ring{k}", [P, D]) for k in range(K)]
        slot_idx = [sb4(f"slot_idx{h}", [P, K // 2], I32) for h in range(2)]
        tab = sb4("tab", [P, WIN], I32)
        tiles_of = sb4("tiles_of", [1, WIN], I32)
        best = sb4("best", [P, NT * D])
        first_step = sb4("first_step", [1, P], I32)

        def tile_loop(eng, body, last=None):
            for k in range(U):
                body(0, k, False)
            with eng.Fori(1, NT // U - (last is not None)) as i:
                for k in range(U):
                    body(i, k, True)
            if last is not None:
                for k in range(U):
                    last(NT // U - 1, k)

        def flat(ap):
            return ap.rearrange("p a b -> p (a b)")

        def group_loop(eng, body):
            body(0, False)
            with eng.Fori(1, NT // U) as i:
                body(i, True)

        class ProjectRows:

            def __init__(self, l):
                self.l = l
                self.in_ready, self.a_ready, self.a_staged, self.idx_ready = (
                    sem(f"{s}_{l}") for s in ("in_ready", "a_ready", "a_staged", "idx_ready"))
                self.stored_before = 16 * (NT // U) * l
                self.a_stored = [gsem(f"a_stored{k}") for k in range(U)]

            def tensor(self, pe):
                def body(i, k, again):
                    pe.wait_ge(self.in_ready, i * U + k + 1)
                    if again:
                        pe.wait_ge(self.a_staged, (i - 1) * U + k + 1)
                    for h in range(H2):
                        mm = pe.matmul(ps[k][:, 0:D], xs[k][:, h, :], w_ab[:, self.l, h, 0:D], start=h == 0, stop=h == 1)
                    mm.then_inc(self.a_ready, 1)
                tile_loop(pe, body)

            def vector(self, dve):
                def body(i, k, again):
                    dve.wait_ge(self.a_ready, i * U + k + 1)
                    if again:
                        dve.wait_ge(self.a_stored[k], self.stored_before + i * 16)
                    dve.tensor_copy(a_st[k][:], ps[k][:, 0:D]).then_inc(self.a_staged, 1)
                tile_loop(dve, body)

            def gpsimd(self, pool):
                def body(i, k, again):
                    if again:
                        hold(pool, self.a_stored[k], self.stored_before + i * 16)
                    pool.tensor_copy(a_idx[k][:], rowid[:, bass.ds(i * U + k, 1)]).then_inc(self.idx_ready, 1)
                    hold(pool, self.idx_ready, i * U + k + 1)
                    hold(pool, self.a_staged, i * U + k + 1)
                    pool.indirect_dma_start(
                        a_rows[self.l], bass.IndirectOffsetOnAxis(ap=a_idx[k][:].bitcast(U32), axis=0),
                        a_st[k][:], None).then_inc(self.a_stored[k], 16)
                tile_loop(pool, body)
                for k in range(U):
                    pool.wait_ge(self.a_stored[k], self.stored_before + 16 * (NT // U))

        class ProjectNodes:

            def __init__(self, l, take_tile):
                self.l, self.take_tile = l, take_tile
                self.xs_ready, self.b_ready, self.b_read = (sem(f"{s}_{l}") for s in ("xs_ready", "b_ready", "b_read"))

            def tensor(self, pe):
                def body(i, k, again):
                    pe.wait_ge(self.xs_ready, i * U + k + 1)
                    if again:
                        pe.wait_ge(self.b_read, (i - 1) * U + k + 1)
                    for h in range(H2):
                        mm = pe.matmul(ps[k][:, 0:D], xs[k][:, h, :], w_ab[:, self.l, h, D:2 * D], start=h == 0,
                                       stop=h == 1)
                    mm.then_inc(self.b_ready, 1)
                tile_loop(pe, body)
                pe.wait_ge(self.b_read, NT)

            def scalar(self, act):
                def body(i, again):
                    for k in range(U):
                        if again:
                            act.wait_ge(self.b_ready, (i - 1) * U + k + 1)
                        self.take_tile(i * U + k, k).then_inc(self.xs_ready, 1)
                    for k in range(U):
                        act.wait_ge(self.b_ready, i * U + k + 1)
                        act.copy(flat(b_rows[:, bass.ds(i * U + k, 1), :]), ps[k][:, 0:D]).then_inc(self.b_read, 1)
                group_loop(act, body)

        c5 = ExitStack()
        c4.callback(c5.close)
        def sb5(name, shape, dt=F32):
            return c5.enter_context(nc.sbuf_tensor(name, shape, dt))
        QC = 400
        NQ = NP // QC
        w_kv = sb5("w_kv", [P, H2, 2 * D])
        w_q = sb5("w_q", [P, H2, D])
        w_o = sb5("w_o", [P, H2, D])
        b_kv = sb5("b_kv", [1, 2 * D])
        b_q = sb5("b_q", [P, H2])
        nb_q = sb5("nb_q", [P, H2])
        b_o = sb5("b_o", [P, H2])
        same = sb5("same", [P, P])
        kv_bd = sb5("kv_bd", [P, H2, P])
        ks_bd = sb5("ks_bd", [P, H2, P])
        ks_col = sb5("ks_col", [P, H2])
        ones_row = sb5("ones_row", [1, P])
        q_pos = sb5("q_pos", [P, H2, QC])
        q_exp = sb5("q_exp", [P, H2, QC])
        den = sb5("den", [P, H2, QC])
        quot = sb5("quot", [P, H2, QC])
        k_pos = [sb5(f"k_pos{k}", [P, D]) for k in range(U)]
        k_exp = [sb5(f"k_exp{k}", [P, D]) for k in range(U)]
        vf = [sb5(f"vf{k}", [P, H2, P + 1]) for k in range(U)]

        loaded3, x_loaded, neg_made, neg_stored = sem("loaded3"), sem("x_loaded"), sem("neg_made"), sem("neg_stored")
        w_sub, w_turned, w_copied = sem("w_sub"), sem("w_turned"), sem("w_copied")
        dve3, norm_ready, x_turned, x_copied = sem("dve3"), sem("norm_ready"), sem("x_turned"), sem("x_copied")
        var_ready, std_ready = sem("var_ready"), sem("std_ready")
        LOADS3 = 16 * (10 + 2 * LAYERS)

        with ExitStack() as c6:
            def sb6(name, shape, dt=F32):
                return c6.enter_context(nc.sbuf_tensor(name, shape, dt))
            th = sb6("th", [P, LAYERS, H2, D])
            ph = sb6("ph", [P, LAYERS, H2, D])
            neg_row = sb6("neg_row", [1, D])
            xr = [sb6(f"xr{k}", [P, D]) for k in range(U)]
            id_f = sb6("id_f", [P, NT])
            id_g = sb6("id_g", [P, NT])
            stats = sb6("stats", [P, NT, 6])
            mv = sb6("mv", [P, NT, 2])
            rstd = sb6("rstd", [P, NT])

            with nc.Block() as block:
                @block.sync
                def _(sp):
                    sp.dma_start(xin[:], x_perm.rearrange("(h p) d -> p h d", p=P)).then_inc(x_loaded, 16)
                    r = "l (h p) i -> p l h i"
                    for l in range(LAYERS):
                        sp.dma_start(th[:, l], t["L0_gnn_thetas"][l].rearrange("(h p) i -> p h i", p=P)).then_inc(loaded3, 16)
                        sp.dma_start(ph[:, l], t["L0_gnn_phis"][l].rearrange("(h p) i -> p h i", p=P)).then_inc(loaded3, 16)
                    r = "(h p) o -> p h o"
                    sp.dma_start(w_kv[:, :, 0:D], t["L0_mix_wk"].rearrange(r, p=P)).then_inc(loaded3, 16)
                    sp.dma_start(w_kv[:, :, D:2 * D], t["L0_mix_wv"].rearrange(r, p=P)).then_inc(loaded3, 16)
                    sp.dma_start(w_q[:], t["L0_mix_wq"].rearrange(r, p=P)).then_inc(loaded3, 16)
                    sp.dma_start(w_o[:], t["L0_mix_wo"].rearrange(r, p=P)).then_inc(loaded3, 16)
                    sp.dma_start(b_kv[:, 0:D], t["L0_mix_bk"].partition_broadcast(1)).then_inc(loaded3, 16)
                    sp.dma_start(b_kv[:, D:2 * D], t["L0_mix_bv"].partition_broadcast(1)).then_inc(loaded3, 16)
                    r = "(h p) -> p h"
                    sp.dma_start(b_o[:], t["L0_mix_bo"].rearrange(r, p=P), allow_slow_non_contiguous=True
                                 ).then_inc(loaded3, 16)
                    sp.dma_start(b_q[:], t["L0_mix_bq"].rearrange(r, p=P), allow_slow_non_contiguous=True
                                 ).then_inc(loaded3, 16)
                    for i, name in enumerate(("L0_gnn_gammas", "L0_gnn_betas")):
                        sp.dma_start(bn_w[:, i], t[name].rearrange("l (h p) -> p l h", p=P),
                                     allow_slow_non_contiguous=True).then_inc(loaded3, 16)
                    sp.wait_ge(neg_made, 1)
                    for l in range(LAYERS):
                        sp.dma_start(a_rows[l][MID:MID + 1, :], neg_row[:]).then_inc(neg_stored, 16)
                    sp.wait_ge(neg_stored, 16 * LAYERS)
                    sp.wait_ge(loaded3, LOADS3)

                @block.tensor
                def _(pe):
                    pe.wait_ge(w_sub, 1)
                    for n in range(2 * LAYERS):
                        if n >= U:
                            pe.wait_ge(w_copied, n - U + 1)
                        w = (th, ph)[n % 2]
                        for ih in range(H2):
                            for oh in range(H2):
                                mm = pe.transpose(ps[n % U][:, ih * D + oh * P:ih * D + (oh + 1) * P],
                                                  w[:, n // 2, oh, ih * P:(ih + 1) * P], ident[:])
                        mm.then_inc(w_turned, 1)
                    pe.wait_ge(w_copied, 2 * LAYERS)

                    def body(i, k, again):
                        pe.wait_ge(norm_ready, i * U + k + 1)
                        if again:
                            pe.wait_ge(x_copied, (i - 1) * U + k + 1)
                        for h in range(H2):
                            mm = pe.transpose(ps[k][:, h * P:(h + 1) * P], xr[k][:, h * P:(h + 1) * P], ident[:])
                        mm.then_inc(x_turned, 1)
                    tile_loop(pe, body)

                @block.scalar
                def _(act):
                    act.wait_ge(var_ready, 1)
                    act.activation(rstd[:], rstd[:], ACT.Sqrt).then_inc(std_ready, 1)
                    for n in range(2 * LAYERS):
                        act.wait_ge(w_turned, n + 1)
                        j = n % 2
                        act.copy(w_ab[:, n // 2, :, j * D:(j + 1) * D],
                                 ps[n % U][:].rearrange("p (h o) -> p h o", h=H2)).then_inc(w_copied, 1)

                    def body(i, k, again):
                        act.wait_ge(x_turned, i * U + k + 1)
                        act.copy(f_t[:, :, bass.ds((i * U + k) * P, P)],
                                 ps[k][:, 0:D].rearrange("p (h q) -> p h q", h=H2)).then_inc(x_copied, 1)
                    tile_loop(act, body)

                @block.vector
                def _(dve):
                    dve.memset(neg_row[:], NEG).then_inc(neg_made, 1)
                    dve.wait_ge(loaded3, LOADS3)
                    dve.tensor_scalar(nb_q[:], b_q[:], -1.0, None, ALU.mult)
                    dve.tensor_tensor(ph[:], ph[:], th[:], ALU.subtract).then_inc(w_sub, 1)
                    dve.wait_ge(x_loaded, 16)
                    ids = xin[:, :, D:D + 1].bitcast(I32).rearrange("p t o -> p (t o)")
                    dve.tensor_copy(rowid[:], ids)
                    dve.tensor_copy(id_f[:], ids).then_inc(dve3, 1)
                    dve.wait_ge(dve3, 1)
                    dve.tensor_scalar(id_g[:], id_f[:], float(MID), None, ALU.is_gt).then_inc(dve3, 1)
                    for n in range(NT):
                        dve.bn_stats(stats[:, n, :], xin[:, n, 0:D])
                    dve.memset(kv_bd[:], 0.0)
                    dve.memset(ones_row[:], 1.0).then_inc(dve3, 1)
                    dve.wait_ge(dve3, 3)
                    dve.tensor_tensor(nodeid[:], id_f[:], id_g[:], ALU.subtract)
                    for n in range(NT):
                        ins = dve.bn_aggr(mv[:, n, :], stats[:, n, :])
                    ins.then_inc(dve3, 1)
                    dve.wait_ge(dve3, 4)
                    dve.tensor_scalar(rstd[:], mv[:, :, 1], EPS, None, ALU.add).then_inc(var_ready, 1)
                    dve.memset(same[:], 0.0).then_inc(dve3, 1)
                    dve.wait_ge(dve3, 5)
                    dve.wait_ge(std_ready, 1)
                    dve.reciprocal(rstd[:], rstd[:]).then_inc(dve3, 1)
                    dve.wait_ge(dve3, 6)
                    for q in range(P // DH):
                        dve.memset(same[q * DH:(q + 1) * DH, q * DH:(q + 1) * DH], 1.0)
                    for k in range(U):
                        dve.memset(vf[k][:, :, P:P + 1], 1.0)

                    def body(i, k, again):
                        n = i * U + k
                        if again:
                            dve.wait_ge(x_turned, (i - 1) * U + k + 1)
                        dve.tensor_scalar(xr[k][:], flat(xin[:, bass.ds(n, 1), 0:D]),
                                          flat(mv[:, bass.ds(n, 1), 0:1]), rstd[:, bass.ds(n, 1)],
                                          ALU.subtract, ALU.mult).then_inc(norm_ready, 1)
                    tile_loop(dve, body)

        rows0 = ProjectRows(0)
        with nc.Block() as block:
            @block.scalar
            def _(act):
                def body(i, k, again):
                    if again:
                        act.wait_ge(rows0.a_ready, (i - 1) * U + k + 1)
                    act.copy(xs[k][:], f_t[:, :, bass.ds((i * U + k) * P, P)]).then_inc(rows0.in_ready, 1)
                tile_loop(act, body)

            block.tensor(rows0.tensor)
            block.vector(rows0.vector)
            block.gpsimd(rows0.gpsimd)

        end_phase()

        HK = K // 2

        class Attention:

            def __init__(self):
                (self.in_ready, self.kv_ready, self.kv_read, self.k_neg, self.k_done, self.kv_used, self.kv_sum,
                 self.ks_read, self.kv_set) = (sem(s) for s in (
                     "kv_in_ready", "kv_ready", "kv_read", "k_neg", "k_done", "kv_used", "kv_sum", "ks_read", "kv_set"))
                (self.q_ready, self.q_neg, self.q_done, self.nd_ready, self.den_set, self.quot_ready, self.o_ready,
                 self.o_read) = (sem(s) for s in (
                     "q_ready", "q_neg", "q_done", "nd_ready", "den_set", "quot_ready", "o_ready", "o_read"))

            def tensor(self, pe):
                def kv_body(i, again, last=False):
                    for k in range(U):
                        pe.wait_ge(self.in_ready, i * U + k + 1)
                        if again:
                            pe.wait_ge(self.kv_read, (i - 1) * U + k + 1)
                        for h in range(H2):
                            pe.matmul(ps[k][:], xs[k][:, h, :], w_kv[:, h, :], start=h == 0, stop=False)
                        pe.matmul(ps[k][:], ones_row[:], b_kv[:], start=False, stop=True).then_inc(self.kv_ready, 1)
                    for k in range(U):
                        rows = LAST if last and k == U - 1 else P
                        pe.wait_ge(self.k_done, i * U + k + 1)
                        for g in range(H2):
                            for term in (k_pos, k_exp):
                                first = not again and k == 0 and g == 0 and term is k_pos
                                mm = pe.matmul(ps[7][:, g * (P + 1):(g + 1) * (P + 1)],
                                               term[k][0:rows, g * P:(g + 1) * P], vf[k][0:rows, g, :], start=first,
                                               stop=last and k == U - 1, skip_group_check=True)
                        mm.then_inc(self.kv_used, 1)
                kv_body(0, False)
                with pe.Fori(1, NT // U - 1) as i:
                    kv_body(i, True)
                kv_body(NT // U - 1, True, True)

                def query(i, again):
                    for o in range(H2):
                        if again:
                            pe.wait_ge(self.q_done, (i - 1) * H2 + o + 1)
                        for h in range(H2):
                            mm = pe.matmul(ps[o][:, 0:QC], w_q[:, h, o * P:(o + 1) * P],
                                           f_t[:, h, bass.ds(i * QC, QC)], start=h == 0, stop=h == 1)
                        mm.then_inc(self.q_ready, 1)

                def chunk(i, again):
                    query(i, again)
                    for g in range(H2):
                        pe.wait_ge(self.q_done, i * H2 + g + 1)
                        if again:
                            pe.wait_ge(self.quot_ready, (i - 1) * H2 + g + 1)
                        for bank, w in ((2 + 2 * g, kv_bd), (3 + 2 * g, ks_bd)):
                            pe.matmul(ps[bank][:, 0:QC], w[:, g, :], q_pos[:, g, :], start=True, stop=False)
                            mm = pe.matmul(ps[bank][:, 0:QC], w[:, g, :], q_exp[:, g, :], start=False, stop=True)
                        mm.then_inc(self.nd_ready, 1)
                    pe.wait_ge(self.quot_ready, i * H2 + 2)
                    for o in range(H2):
                        if again:
                            pe.wait_ge(self.o_read, (i - 1) * H2 + o + 1)
                        for g in range(H2):
                            mm = pe.matmul(ps[6 + o][:, 0:QC], w_o[:, g, o * P:(o + 1) * P], quot[:, g, :],
                                           start=g == 0, stop=g == 1)
                        mm.then_inc(self.o_ready, 1)
                pe.wait_ge(self.kv_read, NT)
                pe.wait_ge(self.kv_set, 1)
                chunk(0, False)
                with pe.Fori(1, NQ) as i:
                    chunk(i, True)

            def scalar(self, act):
                def kv_body(i, again):
                    for k in range(U):
                        if again:
                            act.wait_ge(self.kv_ready, (i - 1) * U + k + 1)
                        act.copy(xs[k][:], f_t[:, :, bass.ds((i * U + k) * P, P)]).then_inc(self.in_ready, 1)
                    for k in range(U):
                        act.wait_ge(self.kv_ready, i * U + k + 1)
                        if again:
                            act.wait_ge(self.kv_used, (i - 1) * U + k + 1)
                        act.copy(vf[k][:, :, 0:P], ps[k][:, D:2 * D].rearrange("p (g e) -> p g e", g=H2))
                        act.activation(k_pos[k][:], ps[k][:, 0:D], ACT.Relu)
                        act.activation(k_exp[k][:], ps[k][:, 0:D], ACT.Relu, scale=-1.0).then_inc(self.kv_read, 1)
                    for k in range(U):
                        act.wait_ge(self.kv_read, i * U + k + 1)
                        act.activation(k_exp[k][:], k_exp[k][:], ACT.Exp, scale=-1.0).then_inc(self.k_done, 1)
                group_loop(act, kv_body)
                act.wait_ge(self.kv_used, NT)
                for g in range(H2):
                    act.copy(ks_col[:, g:g + 1], ps[7][:, g * (P + 1) + P:(g + 1) * (P + 1)]).then_inc(self.ks_read, 1)
                    for q in range(P // DH):
                        head = slice(q * DH, (q + 1) * DH)
                        act.copy(kv_bd[head, g, head], ps[7][head, g * (P + 1) + q * DH:g * (P + 1) + (q + 1) * DH])
                act.wait_ge(self.ks_read, H2)
                for g in range(H2):
                    ins = act.activation(ks_bd[:, g, :], same[:], ACT.Identity, scale=ks_col[:, g:g + 1])
                ins.then_inc(self.kv_set, 1)

                def chunk(i, again):
                    for o in range(H2):
                        act.wait_ge(self.q_ready, i * H2 + o + 1)
                        if again:
                            act.wait_ge(self.nd_ready, (i - 1) * H2 + o + 1)
                        act.activation(q_pos[:, o, :], ps[o][:, 0:QC], ACT.Relu, bias=b_q[:, o:o + 1])
                        act.activation(q_exp[:, o, :], ps[o][:, 0:QC], ACT.Relu, bias=nb_q[:, o:o + 1], scale=-1.0
                                       ).then_inc(self.q_neg, 1)
                    for o in range(H2):
                        act.wait_ge(self.q_neg, i * H2 + o + 1)
                        act.activation(q_exp[:, o, :], q_exp[:, o, :], ACT.Exp, scale=-1.0).then_inc(self.q_done, 1)
                    for o in range(H2):
                        act.wait_ge(self.o_ready, i * H2 + o + 1)
                        act.activation(f_t[:, o, bass.ds(i * QC, QC)], ps[6 + o][:, 0:QC], ACT.Identity,
                                       bias=b_o[:, o:o + 1]).then_inc(self.o_read, 1)
                chunk(0, False)
                with act.Fori(1, NQ) as i:
                    chunk(i, True)

            def divide(self, dve, i, g, again):
                n = i * H2 + g
                dve.wait_ge(self.nd_ready, n + 1)
                if again:
                    dve.wait_ge(self.o_ready, i * H2)
                dve.tensor_scalar(den[:, g, :], ps[3 + 2 * g][:, 0:QC], 1e-6, None, ALU.add).then_inc(self.den_set, 1)
                dve.wait_ge(self.den_set, 2 * n + 1)
                dve.reciprocal(den[:, g, :], den[:, g, :]).then_inc(self.den_set, 1)
                dve.wait_ge(self.den_set, 2 * n + 2)
                dve.tensor_tensor(quot[:, g, :], ps[2 + 2 * g][:, 0:QC], den[:, g, :], ALU.mult
                                  ).then_inc(self.quot_ready, 1)

        ALONE = 16
        assert ALONE + 4 * NQ < -(-NE // (P * K)) and ALONE + 4 * NQ < WIN // K
        for l in range(LAYERS):
            best_set, tab_loaded, idx_set, used, win_over = (
                sem(f"{s}_{l}") for s in ("best_set", "tab_loaded", "idx_set", "used", "win_over"))
            landed = [gsem(f"landed{k}_{l}") for k in range(K)]
            if l == 0:
                attention = Attention()
                nodes = ProjectNodes(0, lambda n, k: nc.scalar.copy(xs[k][:], f_t[:, :, bass.ds(n * P, P)]))
            else:
                nodes = ProjectNodes(l, apply_norm)
            with nc.Block() as block:
                @block.tensor
                def _(pe):
                    nodes.tensor(pe)
                    if l == 0:
                        attention.tensor(pe)

                @block.scalar
                def _(act):
                    nodes.scalar(act)
                    if l == 0:
                        attention.scalar(act)

                @block.sync
                def _(sp):
                    windows = sp.value_load(nwin[0:1, 0:1], min_val=1, max_val=NW)
                    with sp.Fori(0, windows) as w:
                        hold(sp, win_over, w + 1)
                        sp.dma_start(tab[:], table_dram[bass.ds(w, 1)].rearrange("o p g -> (o p) g")
                                     ).then_inc(tab_loaded, 16)
                        sp.dma_start(tiles_of[:], tile_dram[bass.ds(w, 1)]).then_inc(tab_loaded, 16)

                @block.gpsimd
                def _(pool):
                    windows = pool.value_load(nwin[0:1, 0:1], min_val=1, max_val=NW)
                    with pool.Fori(0, windows) as w:
                        hold(pool, tab_loaded, w * 32 + 32)
                        steps = pool.value_load(nstep[0:1, bass.ds(w, 1)], min_val=1, max_val=WIN // K)
                        with pool.Fori(0, steps) as c:
                            gc = w * (WIN // K) + c
                            for h in range(2):
                                hold(pool, used, gc * K + (h + 1) * HK)
                                pool.tensor_copy(slot_idx[h][:], tab[:, bass.ds(c * K + h * HK, HK)]
                                                 ).then_inc(idx_set, 1)
                                hold(pool, idx_set, gc * 2 + h + 1)
                                for k in range(HK):
                                    pool.indirect_dma_start(
                                        ring[h * HK + k][:], None, a_rows[l],
                                        bass.IndirectOffsetOnAxis(ap=slot_idx[h][:, k:k + 1].bitcast(U32), axis=0)
                                    ).then_inc(landed[h * HK + k], 16)

                @block.vector
                def _(dve):
                    windows = dve.value_load(nwin[0:1, 0:1], min_val=1, max_val=NW)
                    def gather_step(w, c):
                        gc = w * (WIN // K) + c
                        _, offs = nc.values_load_multi_w_load_instructions(
                            tiles_of[0:1, bass.ds(c * K, K)], engines=[mybir.EngineType.DVE],
                            min_val=0, max_val=(NT - 1) * D)
                        for k in range(K):
                            m = best[:, bass.ds(offs[k], D)]
                            dve.wait_ge(landed[k], gc * 16 + 16)
                            dve.wait_ge(used, gc * K + K + k)
                            dve.tensor_tensor(m, m, ring[k][:], ALU.max).then_inc(used, 1)

                    dve.memset(first_step[:, 0:1], ALONE + 4 * NQ if l == 0 else 0)
                    dve.memset(first_step[:, 1:P], 0)
                    dve.memset(best[:], NEG).then_inc(used, K)
                    dve.sem_inc(win_over, 1)
                    dve.wait_ge(used, K)
                    if l == 0:
                        dve.wait_ge(tab_loaded, 32)
                        with dve.Fori(0, ALONE) as c:
                            gather_step(0, c)

                        def chunk(i, again):
                            for s in range(4):
                                gather_step(0, ALONE + i * 4 + s)
                                if s % 2 == 0:
                                    attention.divide(dve, i, s // 2, again)
                        chunk(0, False)
                        with dve.Fori(1, NQ) as i:
                            chunk(i, True)
                    with dve.Fori(0, windows) as w:
                        dve.wait_ge(tab_loaded, w * 32 + 32)
                        steps = dve.value_load(nstep[0:1, bass.ds(w, 1)], min_val=1, max_val=WIN // K)
                        done = dve.value_load(first_step[0:1, bass.ds(w, 1)], min_val=0, max_val=ALONE + 4 * NQ)
                        with dve.Fori(done, steps) as c:
                            gather_step(w, c)
                        dve.sem_inc(win_over, 1)

            if l == 0:
                c5.close()
                agg_t = sb4("agg_t", [P, H2, NP])
                st = [sb4(f"st{k}", [P, D]) for k in range(U)]
            sum_ready, sum_turned, agg_copied, dve5 = (
                sem(f"{s}_{l}") for s in ("sum_ready", "sum_turned", "agg_copied", "dve5"))
            bn_ready, bvar_ready, bstd_ready = (sem(f"{s}_{l}") for s in ("bn_ready", "bvar_ready", "bstd_ready"))
            bstats = sb4(f"bstats_{l}", [P, H2, 7, 6])
            bmv = sb4(f"bmv_{l}", [P, H2, 2])
            scale = sb4(f"scale_{l}", [P, H2])
            shift = sb4(f"shift_{l}", [P, H2])
            rows = ProjectRows(l + 1) if l + 1 < LAYERS else None

            def apply_norm(n, k, scale=scale, shift=shift):
                for h in range(H2):
                    ins = nc.scalar.activation(xs[k][:, h, :], agg_t[:, h, bass.ds(n * P, P)], ACT.Relu,
                                               bias=shift[:, h:h + 1], scale=scale[:, h:h + 1])
                return ins
            if rows is None:
                y_ready, y_turned, y_added = sem("y_ready"), sem("y_turned"), sem("y_added")
                out_ready = sem("out_ready")
            with nc.Block() as block:
                @block.tensor
                def _(pe):
                    def body(i, k, again):
                        pe.wait_ge(sum_ready, i * U + k + 1)
                        if again:
                            pe.wait_ge(agg_copied, (i - 1) * U + k + 1)
                        for h in range(H2):
                            mm = pe.transpose(ps[k][:, h * P:(h + 1) * P], st[k][:, h * P:(h + 1) * P], ident[:])
                        mm.then_inc(sum_turned, 1)
                    tile_loop(pe, body)
                    pe.wait_ge(agg_copied, NT)
                    if rows:
                        rows.tensor(pe)
                    else:
                        def body(i, k, again):
                            pe.wait_ge(out_ready, i * U + k + 1)
                            if again:
                                pe.wait_ge(y_added, (i - 1) * U + k + 1)
                            for h in range(H2):
                                mm = pe.transpose(ps[k][:, h * P:(h + 1) * P], xs[k][:, h, :], ident[:])
                            mm.then_inc(y_turned, 1)
                        tile_loop(pe, body)

                @block.scalar
                def _(act):
                    def body(i, k, again):
                        act.wait_ge(sum_turned, i * U + k + 1)
                        act.activation(agg_t[:, :, bass.ds((i * U + k) * P, P)],
                                       ps[k][:, 0:D].rearrange("p (h q) -> p h q", h=H2), ACT.Relu
                                       ).then_inc(agg_copied, 1)
                    tile_loop(act, body)
                    act.wait_ge(bvar_ready, 1)
                    act.activation(scale[:], scale[:], ACT.Sqrt).then_inc(bstd_ready, 1)
                    act.wait_ge(bn_ready, 1)

                    def body(i, k, again):
                        if again:
                            act.wait_ge(rows.a_ready if rows else y_turned, (i - 1) * U + k + 1)
                        apply_norm(i * U + k, k).then_inc(rows.in_ready if rows else y_ready, 1)
                    tile_loop(act, body)

                @block.vector
                def _(dve):
                    def body(i, k, again):
                        if again:
                            dve.wait_ge(sum_turned, (i - 1) * U + k + 1)
                        n = i * U + k
                        dve.tensor_tensor(st[k][:], best[:, bass.ds(n * D, D)], flat(b_rows[:, bass.ds(n, 1), :]),
                                          ALU.add).then_inc(sum_ready, 1)
                    tile_loop(dve, body)
                    dve.wait_ge(agg_copied, NT)
                    count = [0]

                    def step(ins):
                        ins.then_inc(dve5, 1)
                        count[0] += 1
                        dve.wait_ge(dve5, count[0])
                    for h in range(H2):
                        for j in range(7):
                            ins = dve.bn_stats(bstats[:, h, j, :], agg_t[:, h, j * 512:min(j * 512 + 512, N)])
                    step(ins)
                    for h in range(H2):
                        ins = dve.bn_aggr(bmv[:, h, :], flat(bstats[:, h]))
                    step(ins)
                    dve.tensor_scalar(scale[:], bmv[:, :, 1], EPS, None, ALU.add).then_inc(bvar_ready, 1)
                    dve.wait_ge(bstd_ready, 1)
                    step(dve.reciprocal(scale[:], scale[:]))
                    step(dve.tensor_tensor(scale[:], scale[:], bn_w[:, 0, l, :], ALU.mult))
                    step(dve.tensor_tensor(shift[:], bmv[:, :, 0], scale[:], ALU.mult))
                    dve.tensor_tensor(shift[:], bn_w[:, 1, l, :], shift[:], ALU.subtract).then_inc(bn_ready, 1)
                    if rows:
                        rows.vector(dve)
                    else:
                        def body(i, k, again):
                            n = i * U + k
                            dve.wait_ge(y_ready, n + 1)
                            dve.tensor_tensor(xs[k][:], xs[k][:], f_t[:, :, bass.ds(n * P, P)], ALU.add
                                              ).then_inc(out_ready, 1)
                            if k:
                                add(i, k - 1)
                            if k == U - 1:
                                add(i, k)

                        def add(i, k):
                            n = i * U + k
                            dve.wait_ge(y_turned, n + 1)
                            m = flat(xin[:, bass.ds(n, 1), 0:D])
                            dve.tensor_tensor(m, m, ps[k][:, 0:D], ALU.add).then_inc(y_added, 1)
                        tile_loop(dve, body)

                if rows:
                    block.gpsimd(rows.gpsimd)
            end_phase()
        c4.close()

        ET = (2 * N) // P + EXPERTS
        c9 = ExitStack()
        ctx.callback(c9.close)

        def sb9(name, shape, dt=F32):
            return c9.enter_context(nc.sbuf_tensor(name, shape, dt))

        HC = HID // P
        w1 = sb9("w1", [P, EXPERTS, H2, HID])
        w2 = sb9("w2", [P, EXPERTS, HC, D])
        b1 = sb9("b1", [P, EXPERTS, HID])
        b2 = sb9("b2", [P, EXPERTS, D])
        place = [sb9(f"place{i}", [P, NT], I32) for i in range(2)]
        weight = sb9("weight", [P, 2, NT])
        expert_of = sb9("expert_of", [1, 64], I32)
        npairs = sb9("npairs", [1, 1], I32)
        w_loaded, routed, y_stored_all = sem("w_loaded"), sem("routed"), sem("y_stored_all")
        xb_dram = dram("xb_dram", ((ET + 4) * P, D))
        y_dram = dram("y_dram", ((ET + 4) * P, D))
        with ExitStack() as c10:
            def sb10(name, shape, dt=F32):
                return c10.enter_context(nc.sbuf_tensor(name, shape, dt))
            xb = sb10("xb", [P, NT, D])
            w_r = sb10("w_r", [P, H2, EXPERTS])
            b_r = sb10("b_r", [P, EXPERTS])
            gam = sb10("gam", [P, D])
            bet = sb10("bet", [P, D])
            zrow = sb10("zrow", [P, D])
            stats5 = sb10("stats5", [P, 2, NT, 6])
            mv5 = sb10("mv5", [P, 2, NT, 2])
            rstd5 = sb10("rstd5", [P, 2, NT])
            xt5 = [sb10(f"xt5_{k}", [P, H2, P]) for k in range(U)]
            xrow5 = [sb10(f"xrow5_{k}", [P, D]) for k in range(U)]
            logit = sb10("logit", [P, NT, EXPERTS])
            oh = [sb10(f"oh{i}", [P, NT, EXPERTS]) for i in range(2)]
            work = sb10("work", [P, NT, EXPERTS])
            top = [sb10(f"top{i}", [P, NT]) for i in range(2)]
            which = sb10("which", [P, NT])
            valid = sb10("valid", [P, 1])
            before = sb10("before", [P, P])
            ones = sb10("ones", [P, P])
            both = sb10("both", [P, NT, EXPERTS])
            prefix = sb10("prefix", [P, NT + 1, EXPERTS])
            cnt_i = sb10("cnt_i", [P, 2, EXPERTS], I32)
            tiles_f = sb10("tiles_f", [P, EXPERTS])
            tbase = sb10("tbase", [P, EXPERTS + 1])
            place_f = sb10("place_f", [P, NT])
            jcmp = sb10("jcmp", [1, 64, EXPERTS - 1])
            jsum = sb10("jsum", [1, 64])
            jp = sb10("jp", [1, 2])
            jp_i = sb10("jp_i", [1, 2], I32)
            iota_e = sb10("iota_e", [P, EXPERTS])
            iota_j = sb10("iota_j", [1, 64])

            made5, dve5, small_loaded, zero_stored = sem("made5"), sem("dve5x"), sem("small_loaded"), sem("zero_stored")
            var_ready, std_ready, xb_ready, xb_turned, xt_ready, logit_ready, logit_read = (
                sem(s) for s in ("var_ready5", "std_ready5", "xb_ready", "xb_turned", "xt_ready", "logit_ready",
                                 "logit_read"))
            both_ready, counted, diff_ready, exp_ready, placed, sent = (
                (gsem if s == "sent" else sem)(s)
                for s in ("both_ready", "counted", "diff_ready", "exp_ready", "placed", "sent"))
            with nc.Block() as block:
                @block.sync
                def _(sp):
                    sp.dma_start(w_r[:], t["L0_ffn_Wr"].rearrange("(h p) e -> p h e", p=P)).then_inc(small_loaded, 16)
                    sp.dma_start(b_r[:], t["L0_ffn_br"].partition_broadcast(P)).then_inc(small_loaded, 16)
                    sp.dma_start(gam[:], t["L0_ffn_gamma"].partition_broadcast(P)).then_inc(small_loaded, 16)
                    sp.dma_start(bet[:], t["L0_ffn_beta"].partition_broadcast(P)).then_inc(small_loaded, 16)
                    sp.wait_ge(made5, 1)
                    for j in range(0, ET + 4, NT):
                        m = min(NT, ET + 4 - j)
                        sp.dma_start(xb_dram[j * P:(j + m) * P, :].rearrange("(p a) d -> p a d", a=m),
                                     zrow[:].unsqueeze(1).broadcast_to([P, m, D])).then_inc(zero_stored, 16)
                    full = 2 * N // P
                    m = ET + 4 - full
                    sp.dma_start(y_dram[full * P:(ET + 4) * P, :].rearrange("(p a) d -> p a d", a=m),
                                 zrow[:].unsqueeze(1).broadcast_to([P, m, D])).then_inc(zero_stored, 16)
                    for e in range(EXPERTS):
                        sp.dma_start(w1[:, e], t["L0_ffn_W1"][e].rearrange("(h p) o -> p h o", p=P)).then_inc(w_loaded, 16)
                        sp.dma_start(w2[:, e], t["L0_ffn_W2"][e].rearrange("(h p) o -> p h o", p=P)).then_inc(w_loaded, 16)
                    sp.dma_start(flat(b1[:]), t["L0_ffn_b1"].rearrange("e o -> (e o)").partition_broadcast(P)
                                 ).then_inc(w_loaded, 16)
                    sp.dma_start(flat(b2[:]), t["L0_ffn_b2"].rearrange("e o -> (e o)").partition_broadcast(P)
                                 ).then_inc(w_loaded, 16)
                    sp.wait_ge(w_loaded, 16 * (2 * EXPERTS + 2))
                    sp.wait_ge(zero_stored, 16 * (-(-(ET + 4) // NT) + 1))
                    sp.wait_ge(sent, 16 * 2 * NT)

                @block.gpsimd
                def _(pool):
                    pool.memset(zrow[:], 0.0).then_inc(made5, 1)
                    pool.memset(before[:], 1.0).then_inc(made5, 1)
                    pool.wait_ge(made5, 2)
                    pool.affine_select(out=before[:], in_=before[:], compare_op=ALU.is_gt, fill=0.0, base=0,
                                       pattern=[[1, P]], channel_multiplier=-1).then_inc(made5, 1)
                    pool.memset(ones[:], 1.0).then_inc(made5, 1)
                    pool.iota(iota_e[:], [[1, EXPERTS]], base=0, channel_multiplier=0,
                              allow_small_or_imprecise_dtypes=True).then_inc(made5, 1)
                    pool.iota(iota_j[:], [[1, 64]], base=0, channel_multiplier=0,
                              allow_small_or_imprecise_dtypes=True).then_inc(made5, 1)
                    pool.wait_ge(zero_stored, 16 * (-(-(ET + 4) // NT) + 1))
                    pool.wait_ge(placed, 2)
                    for n in range(NT):
                        r = P if n < NT - 1 else LAST
                        for i in range(2):
                            pool.indirect_dma_start(
                                xb_dram, bass.IndirectOffsetOnAxis(ap=place[i][0:r, n:n + 1].bitcast(U32), axis=0),
                                xb[0:r, n, :], None).then_inc(sent, 16)

                @block.tensor
                def _(pe):
                    pe.wait_ge(small_loaded, 64)

                    def front(i, k, again):
                        pe.wait_ge(xb_ready, i * U + k + 1)
                        if again:
                            pe.wait_ge(xt_ready, (i - 1) * U + k + 1)
                        for h in range(H2):
                            mm = pe.transpose(ps[k][:, h * P:(h + 1) * P], xrow5[k][:, h * P:(h + 1) * P],
                                              ident[:])
                        mm.then_inc(xb_turned, 1)

                    def body(i, again):
                        for k in range(U):
                            front(i, k, again)
                        for k in range(U):
                            back(i, k, again)

                    def back(i, k, again):
                        pe.wait_ge(xt_ready, i * U + k + 1)
                        if again:
                            pe.wait_ge(logit_read, (i - 1) * U + k + 1)
                        for h in range(H2):
                            mm = pe.matmul(ps[k][:, D:D + EXPERTS], xt5[k][:, h, :], w_r[:, h, :], start=h == 0,
                                           stop=h == 1)
                        mm.then_inc(logit_ready, 1)
                    group_loop(pe, body)
                    pe.wait_ge(made5, 6)
                    pe.wait_ge(both_ready, 1)
                    pe.matmul(ps[5][:, 0:NT * EXPERTS], before[:], flat(both[:]))
                    pe.matmul(ps[6][:, 0:NT * EXPERTS], ones[:], flat(both[:])).then_inc(counted, 1)

                @block.scalar
                def _(act):
                    for i in range(2):
                        act.wait_ge(var_ready, i + 1)
                        act.activation(rstd5[:, i, :], rstd5[:, i, :], ACT.Sqrt).then_inc(std_ready, 1)

                    def body(i, k, again):
                        n = i * U + k
                        act.wait_ge(xb_turned, n + 1)
                        if again:
                            act.wait_ge(logit_ready, (i - 1) * U + k + 1)
                        act.copy(flat(xt5[k][:]), ps[k][:, 0:D]).then_inc(xt_ready, 1)
                    tile_loop(act, body)
                    act.wait_ge(diff_ready, 1)
                    act.activation(weight[:, 1, :], weight[:, 0, :], ACT.Exp).then_inc(exp_ready, 1)

                @block.vector
                def _(dve):
                    count = [0]

                    def step(ins):
                        ins.then_inc(dve5, 1)
                        count[0] += 1
                        dve.wait_ge(dve5, count[0])
                    dve.wait_ge(small_loaded, 64)
                    for m in range(2):
                        x_in = (xin, xb)[m]
                        for n in range(NT):
                            ins = dve.bn_stats(stats5[:, m, n, :], x_in[:, n, 0:D])
                        step(ins)
                        for n in range(NT):
                            ins = dve.bn_aggr(mv5[:, m, n, :], stats5[:, m, n, :])
                        step(ins)
                        dve.tensor_scalar(rstd5[:, m, :], mv5[:, m, :, 1], EPS, None, ALU.add).then_inc(var_ready, 1)
                        dve.wait_ge(std_ready, m + 1)
                        step(dve.reciprocal(rstd5[:, m, :], rstd5[:, m, :]))
                        for n in range(NT):
                            ins = dve.tensor_scalar(xb[:, n, :], x_in[:, n, 0:D], mv5[:, m, n, 0:1],
                                                    rstd5[:, m, n:n + 1], ALU.subtract, ALU.mult)
                        step(ins)
                    rows3 = [P, NT, D]
                    step(dve.tensor_tensor(xb[:], xb[:], gam[:].unsqueeze(1).broadcast_to(rows3), ALU.mult))
                    step(dve.tensor_tensor(xb[:], xb[:], bet[:].unsqueeze(1).broadcast_to(rows3), ALU.add))

                    def body(i, again):
                        for k in range(U):
                            if again:
                                dve.wait_ge(xb_turned, (i - 1) * U + k + 1)
                            dve.tensor_copy(xrow5[k][:], flat(xb[:, bass.ds(i * U + k, 1), :])).then_inc(xb_ready, 1)
                        for k in range(U):
                            read(i, k)

                    def read(i, k):
                        n = i * U + k
                        dve.wait_ge(logit_ready, n + 1)
                        dve.tensor_tensor(flat(logit[:, bass.ds(n, 1), :]), ps[k][:, D:D + EXPERTS], b_r[:], ALU.add
                                          ).then_inc(logit_read, 1)
                    group_loop(dve, body)
                    dve.wait_ge(logit_read, NT)
                    dve.wait_ge(made5, 6)
                    sh = [P, NT, EXPERTS]
                    e_bc = iota_e[:].unsqueeze(1).broadcast_to(sh)
                    for i in range(2):
                        step(dve.tensor_reduce(top[i][:], logit[:], AX_X, ALU.max))
                        step(dve.tensor_tensor(work[:], logit[:], top[i][:].unsqueeze(2).broadcast_to(sh), ALU.is_lt))
                        step(dve.scalar_tensor_tensor(work[:], work[:], float(EXPERTS), e_bc, ALU.mult, ALU.add))
                        step(dve.tensor_reduce(which[:], work[:], AX_X, ALU.min))
                        step(dve.tensor_tensor(oh[i][:], e_bc, which[:].unsqueeze(2).broadcast_to(sh), ALU.is_equal))
                        if i == 0:
                            step(dve.scalar_tensor_tensor(logit[:], oh[0][:], NEG, logit[:], ALU.mult, ALU.add))
                    step(dve.tensor_scalar(valid[:], iota_p[:], float(LAST), None, ALU.is_lt))
                    for i in range(2):
                        step(dve.tensor_scalar(oh[i][:, NT - 1, :], oh[i][:, NT - 1, :], valid[:, 0:1], None, ALU.mult))
                    dve.tensor_tensor(weight[:, 0, :], top[1][:], top[0][:], ALU.subtract).then_inc(diff_ready, 1)
                    dve.tensor_tensor(both[:], oh[0][:], oh[1][:], ALU.add).then_inc(both_ready, 1)
                    dve.wait_ge(exp_ready, 1)
                    step(dve.tensor_scalar(weight[:, 0, :], weight[:, 1, :], 1.0, None, ALU.add))
                    step(dve.reciprocal(weight[:, 0, :], weight[:, 0, :]))
                    step(dve.tensor_tensor(weight[:, 1, :], weight[:, 1, :], weight[:, 0, :], ALU.mult))
                    dve.wait_ge(counted, 1)
                    step(dve.memset(prefix[:], 0.0))
                    step(dve.tensor_copy(work[:], ps[6][:, 0:NT * EXPERTS].rearrange("p (a b) -> p a b", b=EXPERTS)))
                    zcol = prefix[:, 0:1, 0:1].rearrange("p a b -> p (a b)").broadcast_to([P, NT])
                    for e in range(EXPERTS):
                        ins = dve.tensor_tensor_scan(prefix[:, 1:NT + 1, e], work[:, :, e], zcol, 0.0, ALU.add, ALU.add)
                    step(ins)
                    step(dve.tensor_scalar(tiles_f[:], prefix[:, NT, :], float(P - 1), None, ALU.add))
                    step(dve.tensor_copy(cnt_i[:, 0, :], tiles_f[:]))
                    step(dve.tensor_scalar(cnt_i[:, 1, :], cnt_i[:, 0, :], 7, None, ALU.logical_shift_right))
                    step(dve.tensor_copy(tiles_f[:], cnt_i[:, 1, :]))
                    step(dve.memset(tbase[:], 0.0))
                    step(dve.tensor_tensor_scan(tbase[:, 1:EXPERTS + 1], tiles_f[:], zcol[:, 0:EXPERTS], 0.0, ALU.add, ALU.add))
                    step(dve.scalar_tensor_tensor(work[:], tbase[:, 0:EXPERTS].unsqueeze(1).broadcast_to(sh), float(P),
                                                  prefix[:, 0:NT, :], ALU.mult, ALU.add))
                    step(dve.tensor_tensor(work[:], work[:], ps[5][:, 0:NT * EXPERTS].rearrange(
                        "p (a b) -> p a b", b=EXPERTS), ALU.add))
                    for i in range(2):
                        step(dve.tensor_tensor(oh[i][:], oh[i][:], work[:], ALU.mult))
                        step(dve.tensor_reduce(place_f[:], oh[i][:], AX_X, ALU.add))
                        step(dve.tensor_copy(place[i][:], place_f[:]))
                        dve.sem_inc(placed, 1)
                    shj = [1, 64, EXPERTS - 1]
                    step(dve.tensor_tensor(jcmp[:], tbase[0:1, 1:EXPERTS].unsqueeze(1).broadcast_to(shj),
                                           iota_j[:].unsqueeze(2).broadcast_to(shj), ALU.is_le))
                    step(dve.tensor_reduce(jsum[:], jcmp[:], AX_X, ALU.add))
                    step(dve.tensor_copy(expert_of[:], jsum[:]))
                    step(dve.tensor_scalar(jp[:, 0:1], tbase[0:1, EXPERTS:EXPERTS + 1], 1.0, None, ALU.add))
                    step(dve.tensor_copy(jp_i[:, 0:1], jp[:, 0:1]))
                    step(dve.tensor_scalar(npairs[:], jp_i[:, 0:1], 1, None, ALU.logical_shift_right))

        with ExitStack() as c11:
            def ring2(name, shape):
                return [c11.enter_context(nc.sbuf_tensor(f"{name}{k}", shape, F32)) for k in range(2)]
            row5 = ring2("row5_", [P, D])
            xt = ring2("xt", [P, H2, P])
            hb = ring2("hb", [P, HID])
            hg = ring2("hg", [P, HID])
            ht = ring2("ht", [P, HC, P])
            yo = ring2("yo", [P, D])
            row_loaded = [sem(f"row_loaded{k}") for k in range(2)]
            y_stored = [sem(f"y_stored{k}") for k in range(2)]
            xt_turned, xt_ready, h_ready, h_biased, h_done, h_turned, ht_ready, y_ready, y_biased = (
                sem(s) for s in ("xt_turned6", "xt_ready6", "h_ready", "h_biased", "h_done", "h_turned", "ht_ready",
                                 "y_ready6", "y_biased"))

            def past(eng, semaphore, value):
                if not isinstance(value, int) or value > 0:
                    eng.wait_ge(semaphore, value)

            def expert(eng, j):
                return eng.value_load(expert_of[0:1, bass.ds(j, 1)], min_val=0, max_val=EXPERTS - 1)

            def pair_loop(eng, step):
                pairs = eng.value_load(npairs[0:1, 0:1], min_val=2, max_val=ET // 2)
                for j in range(2):
                    step(j, j)
                with eng.Fori(1, pairs) as c:
                    for k in range(2):
                        step(2 * c + k, k)

            with nc.Block() as block:
                @block.sync
                def _(sp):
                    def load(j, k):
                        if not isinstance(j, int) or j >= 2:
                            hold(sp, xt_turned, j - 1)
                        sp.dma_start(row5[k][:], xb_dram[bass.ds(j * P, P), :]).then_inc(row_loaded[k], 16)

                    def step(j, k):
                        load(j + 4, k)
                        hold(sp, y_biased, j + 1)
                        sp.dma_start(y_dram[bass.ds(j * P, P), :], yo[k][:]).then_inc(y_stored[k], 16)
                    for j in range(4):
                        load(j, j % 2)
                    pair_loop(sp, step)
                    pairs = sp.value_load(npairs[0:1, 0:1], min_val=2, max_val=ET // 2)
                    for k in range(2):
                        hold(sp, row_loaded[k], pairs * 16 + 32)
                        hold(sp, y_stored[k], pairs * 16)

                @block.tensor
                def _(pe):
                    def turn_x(j, k):
                        pe.wait_ge(row_loaded[k], (j - k) * 8 + 16)
                        past(pe, xt_ready, j - 1)
                        for h in range(H2):
                            mm = pe.transpose(ps[k][:, h * P:(h + 1) * P], row5[k][:, h * P:(h + 1) * P], ident[:])
                        mm.then_inc(xt_turned, 1)

                    def hidden(j, k, e):
                        pe.wait_ge(xt_ready, j + 1)
                        past(pe, h_biased, j - 1)
                        for h in range(H2):
                            mm = pe.matmul(ps[2 + k][:], xt[k][:, h, :],
                                           w1[:, bass.ds(e, 1), h, :].rearrange("p a o -> p (a o)"),
                                           start=h == 0, stop=h == 1)
                        mm.then_inc(h_ready, 1)

                    def step(j, k):
                        e_next, e = expert(pe, j + 2), expert(pe, j)
                        pe.wait_ge(h_done, j + 1)
                        past(pe, ht_ready, j - 1)
                        for h in range(HC):
                            mm = pe.transpose(ps[4 + k][:, h * P:(h + 1) * P], hg[k][:, h * P:(h + 1) * P], ident[:])
                        mm.then_inc(h_turned, 1)
                        hidden(j + 2, k, e_next)
                        turn_x(j + 3, 1 - k)
                        pe.wait_ge(ht_ready, j + 1)
                        past(pe, y_biased, j - 1)
                        for h in range(HC):
                            mm = pe.matmul(ps[6 + k][:, 0:D], ht[k][:, h, :],
                                           w2[:, bass.ds(e, 1), h, :].rearrange("p a o -> p (a o)"),
                                           start=h == 0, stop=h == HC - 1)
                        mm.then_inc(y_ready, 1)
                    turn_x(0, 0)
                    turn_x(1, 1)
                    hidden(0, 0, expert(pe, 0))
                    hidden(1, 1, expert(pe, 1))
                    turn_x(2, 0)
                    pair_loop(pe, step)

                @block.scalar
                def _(act):
                    def copy_x(j, k):
                        act.wait_ge(xt_turned, j + 1)
                        past(act, h_ready, j - 1)
                        act.copy(flat(xt[k][:]), ps[k][:, 0:D]).then_inc(xt_ready, 1)

                    def gelu(j, k):
                        act.wait_ge(h_biased, j + 1)
                        past(act, h_turned, j - 1)
                        act.activation(hg[k][:], hb[k][:], ACT.Gelu).then_inc(h_done, 1)

                    def step(j, k):
                        act.wait_ge(h_turned, j + 1)
                        past(act, y_ready, j - 1)
                        act.copy(flat(ht[k][:]), ps[4 + k][:, 0:HID]).then_inc(ht_ready, 1)
                        gelu(j + 2, k)
                        copy_x(j + 3, 1 - k)
                    copy_x(0, 0)
                    copy_x(1, 1)
                    gelu(0, 0)
                    copy_x(2, 0)
                    gelu(1, 1)
                    pair_loop(act, step)

                @block.vector
                def _(dve):
                    def bias(j, k, e):
                        dve.wait_ge(h_ready, j + 1)
                        past(dve, h_done, j - 1)
                        dve.tensor_tensor(hb[k][:], ps[2 + k][:], flat(b1[:, bass.ds(e, 1), :]), ALU.add
                                          ).then_inc(h_biased, 1)

                    def step(j, k):
                        e_next, e = expert(dve, j + 2), expert(dve, j)
                        bias(j + 2, k, e_next)
                        dve.wait_ge(y_ready, j + 1)
                        past(dve, y_stored[k], (j - k) * 8)
                        dve.tensor_tensor(yo[k][:], ps[6 + k][:, 0:D], flat(b2[:, bass.ds(e, 1), :]), ALU.add
                                          ).then_inc(y_biased, 1)
                    bias(0, 0, expert(dve, 0))
                    bias(1, 1, expert(dve, 1))
                    pair_loop(dve, step)

        with ExitStack() as c12:
            RY = 4
            got = [[c12.enter_context(nc.sbuf_tensor(f"got{i}_{k}", [P, D], F32)) for k in range(RY)] for i in range(2)]
            fetched = [[gsem(f"fetched{i}_{k}") for k in range(RY)] for i in range(2)]
            summed, half, out_stored = sem("summed"), sem("half"), gsem("out_stored")
            with nc.Block() as block:
                @block.gpsimd
                def _(pool):
                    def send(n):
                        r = P if n < NT - 1 else LAST
                        pool.wait_ge(summed, n + 1)
                        pool.indirect_dma_start(
                            out, bass.IndirectOffsetOnAxis(ap=nodeid[0:r, n:n + 1].bitcast(U32), axis=0),
                            xin[0:r, n, 0:D], None).then_inc(out_stored, 16)
                    for n in range(NT):
                        k, r = n % RY, P if n < NT - 1 else LAST
                        if n >= RY:
                            pool.wait_ge(summed, n - RY + 1)
                        for i in range(2):
                            pool.indirect_dma_start(
                                got[i][k][0:r, :], None, y_dram,
                                bass.IndirectOffsetOnAxis(ap=place[i][0:r, n:n + 1].bitcast(U32), axis=0)
                            ).then_inc(fetched[i][k], 16)
                        if n >= RY - 1:
                            send(n - RY + 1)
                    for n in range(NT - RY + 1, NT):
                        send(n)
                    pool.wait_ge(out_stored, 16 * NT)

                @block.vector
                def _(dve):
                    for n in range(NT):
                        k, r = n % RY, P if n < NT - 1 else LAST
                        row = xin[0:r, n, 0:D]
                        dve.wait_ge(fetched[0][k], 16 * (n // RY + 1))
                        dve.scalar_tensor_tensor(row, got[0][k][0:r, :], weight[0:r, 0, n:n + 1], row, ALU.mult, ALU.add
                                                 ).then_inc(half, 1)
                        dve.wait_ge(fetched[1][k], 16 * (n // RY + 1))
                        dve.wait_ge(half, n + 1)
                        dve.scalar_tensor_tensor(row, got[1][k][0:r, :], weight[0:r, 1, n:n + 1], row, ALU.mult, ALU.add
                                                 ).then_inc(summed, 1)


NAMES = ["x", "src", "dst", "L0_gnn_thetas", "L0_gnn_phis", "L0_gnn_gammas", "L0_gnn_betas",
         "L0_mix_wq", "L0_mix_bq", "L0_mix_wk", "L0_mix_bk", "L0_mix_wv", "L0_mix_bv", "L0_mix_wo", "L0_mix_bo",
         "L0_ffn_gamma", "L0_ffn_beta", "L0_ffn_Wr", "L0_ffn_br", "L0_ffn_W1", "L0_ffn_b1", "L0_ffn_W2", "L0_ffn_b2"]


def kernel(**inputs):
    from concourse import bacc
    from concourse.bass_utils import run_bass_kernel_spmd

    nc = bacc.Bacc("TRN2", target_bir_lowering=False, num_devices=1)
    arrays, t = {}, {}
    for name in NAMES:
        a = np.ascontiguousarray(inputs[name])
        arrays[f"in_{name}"] = a
        t[name] = nc.dram_tensor(f"in_{name}", a.shape, mybir.dt.from_np(a.dtype), kind="ExternalInput").ap()
    out = nc.dram_tensor("out", (N, D), F32, kind="ExternalOutput").ap()
    build(nc, t, out)
    return run_bass_kernel_spmd(nc, [arrays], core_ids=[0]).results[0]["out"]
```
